# Optimizing a Trainium2 kernel written in Bass

```python
import numpy as np
import jax
import jax.numpy as jnp

def _softmax(x, axis=-1):
    return jax.nn.softmax(x, axis=axis)

def _gelu(x):
    return jax.nn.gelu(x, approximate=True)

def _silu(x):
    return jax.nn.silu(x)

def _sigmoid(x):
    return jax.nn.sigmoid(x)

def _layernorm(x, axis=-1, eps=1e-05):
    m = jnp.mean(x, axis=axis, keepdims=True)
    v = jnp.var(x, axis=axis, keepdims=True)
    return (x - m) / jnp.sqrt(v + eps)

def _scatter_add(tgt, idx, src, axis=0):
    return tgt.at[idx].add(src)

def _segment_sum(src, seg, n):
    return jax.ops.segment_sum(src, seg, n)
kernel_name = 'mk_decoder_postln_d2_seqx_r8_5637a0'

def setup_inputs(seed: int=0):
    np.random.seed(seed)
    _w = jnp.asarray

    def _rec_inputs():
        import jax
        import jax.numpy as jnp
        _rk = jax.random.key(seed)
        x = -0.0002928 + 1 * jax.random.normal(jax.random.fold_in(_rk, 1), (32, 64, 128), jnp.float32)
        _lenS = 64 - jax.random.randint(jax.random.fold_in(_rk, 7), (32,), 0, max(1, 64 // 4) + 1, jnp.int32)
        _lenS2 = 64 - jax.random.randint(jax.random.fold_in(_rk, 8), (32,), 0, max(1, 64 // 4) + 1, jnp.int32)
        _ctx_1024P = jax.random.normal(jax.random.fold_in(_rk, 11), (32, 16, 128), jnp.float32)
        _ctx_1024c = jax.random.dirichlet(jax.random.fold_in(_rk, 511), 0.3 * jnp.ones((16,), jnp.float32), (32, 64))
        _ctx_1024t = jnp.einsum('bsk,bkd->bsd', _ctx_1024c, _ctx_1024P)
        _ctx_1024t = _ctx_1024t * jax.lax.rsqrt(jnp.mean(jnp.square(_ctx_1024t)) + 1e-12) * 0.953939
        ctx_1024 = -1.39393e-06 + 0.999914 * (_ctx_1024t + 0.3 * jax.random.normal(jax.random.fold_in(_rk, 611), (32, 64, 128), jnp.float32))
        _validS = jnp.arange(64)[None, :] < _lenS[:, None]
        _validS2 = jnp.arange(64)[None, :] < _lenS2[:, None]
        _causal = jnp.tril(jnp.ones((64, 64), dtype=bool))
        mask_BxS2_bf1 = jnp.ones((32, 64), dtype=bool)
        return (x, ctx_1024, mask_BxS2_bf1)
    x, ctx_1024, mask_BxS2_bf1 = _rec_inputs()

    def _L0_attn_setup():
        import jax, jax.numpy as jnp
        import numpy as np
        import math
        HEAD_SIZE = 64

        def rotate_every_two(x):
            x1 = x[..., ::2]
            x2 = x[..., 1::2]
            return jnp.stack((-x2, x1), axis=-1).reshape(x.shape)

        def rope_table(seq_len, dtype=jnp.float32):
            pos = jnp.arange(seq_len, dtype=jnp.float32)
            inv = 10000.0 ** (jnp.arange(0, HEAD_SIZE, 2, dtype=jnp.float32) / HEAD_SIZE)
            radians = pos[:, None] / inv
            sincos = jnp.stack((jnp.sin(radians), jnp.cos(radians)), axis=-1).reshape(seq_len, -1)
            t = jnp.repeat(sincos, 2, axis=-1)
            return t.astype(dtype)
        key = jax.random.key(seed)
        ks = jax.random.split(key, 7)
        B, S, H = (2, 512, 128)
        sd = 1.0 / math.sqrt(H)
        return {'hidden_states': jax.random.normal(ks[0], (B, S, H), dtype=jnp.float32), 'Wq': jax.random.normal(ks[1], (H, H), dtype=jnp.float32) * sd, 'bq': jax.random.normal(ks[2], (H,), dtype=jnp.float32) * sd, 'Wk': jax.random.normal(ks[3], (H, H), dtype=jnp.float32) * sd, 'bk': jax.random.normal(ks[4], (H,), dtype=jnp.float32) * sd, 'Wv': jax.random.normal(ks[5], (H, H), dtype=jnp.float32) * sd, 'bv': jax.random.normal(ks[6], (H,), dtype=jnp.float32) * sd}
    _L0_attn_all = _L0_attn_setup()
    _L0_attn_in = {k: v for k, v in _L0_attn_all.items() if k in ('Wq', 'bq', 'Wk', 'bk', 'Wv', 'bv')}
    del _L0_attn_all

    def _L0_xattn_setup():
        import jax, jax.numpy as jnp
        import numpy as np
        N_HEADS = 16
        D_MODEL = 128
        HEAD_DIM = D_MODEL // N_HEADS
        MASK_FILL = -100000000.0

        def _split_heads(x):
            B, S, _ = x.shape
            return x.reshape(B, S, N_HEADS, HEAD_DIM).transpose(0, 2, 1, 3)
        key = jax.random.key(seed)
        ks = jax.random.split(key, 12)
        B, L, P = (2, 256, 256)
        s = 1.0 / np.sqrt(D_MODEL).astype(np.float32)
        inp = {'q': jax.random.normal(ks[0], (B, L, D_MODEL), dtype=jnp.float32), 'k': jax.random.normal(ks[1], (B, P, D_MODEL), dtype=jnp.float32), 'v': jax.random.normal(ks[2], (B, P, D_MODEL), dtype=jnp.float32), 'attention_mask': jnp.ones((B, P), dtype=bool), 'Wq': jax.random.normal(ks[3], (D_MODEL, D_MODEL), dtype=jnp.float32) * s, 'bq': jnp.zeros((D_MODEL,), dtype=jnp.float32), 'Wk': jax.random.normal(ks[4], (D_MODEL, D_MODEL), dtype=jnp.float32) * s, 'bk': jnp.zeros((D_MODEL,), dtype=jnp.float32), 'Wv': jax.random.normal(ks[5], (D_MODEL, D_MODEL), dtype=jnp.float32) * s, 'bv': jnp.zeros((D_MODEL,), dtype=jnp.float32), 'Wo': jax.random.normal(ks[6], (D_MODEL, D_MODEL), dtype=jnp.float32) * s, 'bo': jnp.zeros((D_MODEL,), dtype=jnp.float32)}
        return inp
    _L0_xattn_all = _L0_xattn_setup()
    _L0_xattn_in = {k: v for k, v in _L0_xattn_all.items() if k in ('Wq', 'bq', 'Wk', 'bk', 'Wv', 'bv', 'Wo', 'bo')}
    del _L0_xattn_all

    def _L0_ffn_setup():
        import jax, jax.numpy as jnp
        import numpy as np
        B, S, H, D, E = (4, 128, 128, 512, 8)
        key = jax.random.key(seed)
        ks = jax.random.split(key, 12)

        def init(k, shape, fan_in):
            return jax.random.normal(k, shape, jnp.float32) / np.float32(np.sqrt(fan_in))
        return {'x': jax.random.normal(ks[0], (B, S, H), jnp.float32), 'Wq': init(ks[1], (H, H), H), 'bq': jnp.zeros((H,), jnp.float32), 'Wk': init(ks[2], (H, H), H), 'bk': jnp.zeros((H,), jnp.float32), 'Wv': init(ks[3], (H, H), H), 'bv': jnp.zeros((H,), jnp.float32), 'Wo': init(ks[4], (H, H), H), 'bo': jnp.zeros((H,), jnp.float32), 'Wg': init(ks[5], (H, E), H), 'bg': jnp.zeros((E,), jnp.float32), 'W1': init(ks[6], (E, H, D), H), 'b1': jnp.zeros((E, D), jnp.float32), 'W2': init(ks[7], (E, D, H), D), 'b2': jnp.zeros((E, H), jnp.float32)}
    _L0_ffn_all = _L0_ffn_setup()
    _L0_ffn_in = {k: v for k, v in _L0_ffn_all.items() if k in ('Wq', 'bq', 'Wk', 'bk', 'Wv', 'bv', 'Wo', 'bo', 'Wg', 'bg', 'W1', 'b1', 'W2', 'b2')}
    del _L0_ffn_all

    def _L1_attn_setup():
        import jax, jax.numpy as jnp
        import numpy as np
        B, S, D = (2, 256, 128)
        H = 16
        HD = D // H
        WINDOW = 128
        SCALE = HD ** (-0.5)

        def _local_mask(seq_len):
            idx = jnp.arange(seq_len)
            band = jnp.abs(idx[:, None] - idx[None, :]) <= WINDOW // 2
            return jnp.where(band, 0.0, -jnp.inf).astype(jnp.float32)
        key = jax.random.key(seed)
        ks = jax.random.split(key, 5)
        x = jax.random.normal(ks[0], (B, S, D), dtype=jnp.float32)
        w_qkv = jax.random.normal(ks[1], (D, 3 * D), dtype=jnp.float32) * D ** (-0.5)
        b_qkv = jax.random.normal(ks[2], (3 * D,), dtype=jnp.float32) * 0.02
        w_out = jax.random.normal(ks[3], (D, D), dtype=jnp.float32) * D ** (-0.5)
        b_out = jax.random.normal(ks[4], (D,), dtype=jnp.float32) * 0.02
        return {'x': x, 'w_qkv': w_qkv, 'b_qkv': b_qkv, 'w_out': w_out, 'b_out': b_out}
    _L1_attn_all = _L1_attn_setup()
    _L1_attn_in = {k: v for k, v in _L1_attn_all.items() if k in ('w_qkv', 'b_qkv', 'w_out', 'b_out')}
    del _L1_attn_all

    def _L1_xattn_setup():
        import jax, jax.numpy as jnp
        import numpy as np
        import math
        EPS = 1e-05

        def _layernorm(x, gamma, beta):
            mu = jnp.mean(x, axis=-1, keepdims=True)
            var = jnp.mean(jnp.square(x - mu), axis=-1, keepdims=True)
            return (x - mu) * jax.lax.rsqrt(var + EPS) * gamma + beta
        key = jax.random.key(seed)
        ks = jax.random.split(key, 8)
        B, Sq, Sk, D = (2, 256, 256, 128)
        s = 1.0 / math.sqrt(D)
        return {'Q': jax.random.normal(ks[0], (B, Sq, D), jnp.float32), 'K': jax.random.normal(ks[1], (B, Sk, D), jnp.float32), 'Wq': jax.random.normal(ks[2], (D, D), jnp.float32) * s, 'bq': jnp.zeros((D,), jnp.float32), 'Wk': jax.random.normal(ks[3], (D, D), jnp.float32) * s, 'bk': jnp.zeros((D,), jnp.float32), 'Wv': jax.random.normal(ks[4], (D, D), jnp.float32) * s, 'bv': jnp.zeros((D,), jnp.float32), 'Wo': jax.random.normal(ks[5], (D, D), jnp.float32) * s, 'bo': jnp.zeros((D,), jnp.float32), 'g0': jnp.ones((D,), jnp.float32), 'b0': jnp.zeros((D,), jnp.float32), 'g1': jnp.ones((D,), jnp.float32), 'b1': jnp.zeros((D,), jnp.float32)}
    _L1_xattn_all = _L1_xattn_setup()
    _L1_xattn_in = {k: v for k, v in _L1_xattn_all.items() if k in ('Wq', 'bq', 'Wk', 'bk', 'Wv', 'bv', 'Wo', 'bo', 'g0', 'b0', 'g1', 'b1')}
    del _L1_xattn_all

    def _L1_ffn_setup():
        import jax, jax.numpy as jnp
        import numpy as np
        JITTER_EPS = 0.01
        NEG_INF = -jnp.inf

        def sparsemixer_eval(scores, jitter_eps):
            m1 = jnp.max(scores, axis=-1, keepdims=True)
            ind1 = jnp.argmax(scores, axis=-1)
            factor1 = jnp.maximum(jnp.abs(scores), m1)
            mask1 = jax.lax.stop_gradient((m1 - scores) / factor1 > 2.0 * jitter_eps)
            gates1 = jax.nn.softmax(jnp.where(mask1, NEG_INF, scores), axis=-1)
            mult1 = jnp.take_along_axis(gates1, ind1[:, None], axis=-1)[:, 0]
            E = scores.shape[-1]
            onehot1 = ind1[:, None] == jnp.arange(E)[None, :]
            masked_scores = jnp.where(onehot1, NEG_INF, scores)
            m2 = jnp.max(masked_scores, axis=-1, keepdims=True)
            ind2 = jnp.argmax(masked_scores, axis=-1)
            factor2 = jnp.maximum(jnp.abs(scores), m2)
            mask2 = jax.lax.stop_gradient((m2 - scores) / factor2 > 2.0 * jitter_eps)
            gates2 = jax.nn.softmax(jnp.where(mask2, NEG_INF, masked_scores), axis=-1)
            mult2 = jnp.take_along_axis(gates2, ind2[:, None], axis=-1)[:, 0]
            multiplier = jnp.stack([mult1, mult2], axis=-1)
            selected = jnp.stack([ind1, ind2], axis=-1)
            return (multiplier, selected)
        key = jax.random.key(seed)
        k0, k1, k2, k3, k4 = jax.random.split(key, 5)
        B, S, H, F, E = (2, 128, 128, 256, 8)
        scale = 0.02
        return {'hidden_states': jax.random.normal(k0, (B, S, H), dtype=jnp.float32), 'router_w': jax.random.normal(k1, (E, H), dtype=jnp.float32) * scale, 'w_gate': jax.random.normal(k2, (E, F, H), dtype=jnp.float32) * scale, 'w_up': jax.random.normal(k3, (E, F, H), dtype=jnp.float32) * scale, 'w_down': jax.random.normal(k4, (E, H, F), dtype=jnp.float32) * scale}
    _L1_ffn_all = _L1_ffn_setup()
    _L1_ffn_in = {k: v for k, v in _L1_ffn_all.items() if k in ('router_w', 'w_gate', 'w_up', 'w_down')}
    del _L1_ffn_all
    return {'x': x, 'ctx_1024': ctx_1024, 'mask_BxS2_bf1': mask_BxS2_bf1, 'L0_attn_Wq': _L0_attn_in['Wq'], 'L0_attn_bq': _L0_attn_in['bq'], 'L0_attn_Wk': _L0_attn_in['Wk'], 'L0_attn_bk': _L0_attn_in['bk'], 'L0_attn_Wv': _L0_attn_in['Wv'], 'L0_attn_bv': _L0_attn_in['bv'], 'L0_xattn_Wq': _L0_xattn_in['Wq'], 'L0_xattn_bq': _L0_xattn_in['bq'], 'L0_xattn_Wk': _L0_xattn_in['Wk'], 'L0_xattn_bk': _L0_xattn_in['bk'], 'L0_xattn_Wv': _L0_xattn_in['Wv'], 'L0_xattn_bv': _L0_xattn_in['bv'], 'L0_xattn_Wo': _L0_xattn_in['Wo'], 'L0_xattn_bo': _L0_xattn_in['bo'], 'L0_ffn_Wq': _L0_ffn_in['Wq'], 'L0_ffn_bq': _L0_ffn_in['bq'], 'L0_ffn_Wk': _L0_ffn_in['Wk'], 'L0_ffn_bk': _L0_ffn_in['bk'], 'L0_ffn_Wv': _L0_ffn_in['Wv'], 'L0_ffn_bv': _L0_ffn_in['bv'], 'L0_ffn_Wo': _L0_ffn_in['Wo'], 'L0_ffn_bo': _L0_ffn_in['bo'], 'L0_ffn_Wg': _L0_ffn_in['Wg'], 'L0_ffn_bg': _L0_ffn_in['bg'], 'L0_ffn_W1': _L0_ffn_in['W1'], 'L0_ffn_b1': _L0_ffn_in['b1'], 'L0_ffn_W2': _L0_ffn_in['W2'], 'L0_ffn_b2': _L0_ffn_in['b2'], 'L1_attn_w_qkv': _L1_attn_in['w_qkv'], 'L1_attn_b_qkv': _L1_attn_in['b_qkv'], 'L1_attn_w_out': _L1_attn_in['w_out'], 'L1_attn_b_out': _L1_attn_in['b_out'], 'L1_xattn_Wq': _L1_xattn_in['Wq'], 'L1_xattn_bq': _L1_xattn_in['bq'], 'L1_xattn_Wk': _L1_xattn_in['Wk'], 'L1_xattn_bk': _L1_xattn_in['bk'], 'L1_xattn_Wv': _L1_xattn_in['Wv'], 'L1_xattn_bv': _L1_xattn_in['bv'], 'L1_xattn_Wo': _L1_xattn_in['Wo'], 'L1_xattn_bo': _L1_xattn_in['bo'], 'L1_xattn_g0': _L1_xattn_in['g0'], 'L1_xattn_b0': _L1_xattn_in['b0'], 'L1_xattn_g1': _L1_xattn_in['g1'], 'L1_xattn_b1': _L1_xattn_in['b1'], 'L1_ffn_router_w': _L1_ffn_in['router_w'], 'L1_ffn_w_gate': _L1_ffn_in['w_gate'], 'L1_ffn_w_up': _L1_ffn_in['w_up'], 'L1_ffn_w_down': _L1_ffn_in['w_down']}

def reference(x, ctx_1024, mask_BxS2_bf1, L0_attn_Wq, L0_attn_bq, L0_attn_Wk, L0_attn_bk, L0_attn_Wv, L0_attn_bv, L0_xattn_Wq, L0_xattn_bq, L0_xattn_Wk, L0_xattn_bk, L0_xattn_Wv, L0_xattn_bv, L0_xattn_Wo, L0_xattn_bo, L0_ffn_Wq, L0_ffn_bq, L0_ffn_Wk, L0_ffn_bk, L0_ffn_Wv, L0_ffn_bv, L0_ffn_Wo, L0_ffn_bo, L0_ffn_Wg, L0_ffn_bg, L0_ffn_W1, L0_ffn_b1, L0_ffn_W2, L0_ffn_b2, L1_attn_w_qkv, L1_attn_b_qkv, L1_attn_w_out, L1_attn_b_out, L1_xattn_Wq, L1_xattn_bq, L1_xattn_Wk, L1_xattn_bk, L1_xattn_Wv, L1_xattn_bv, L1_xattn_Wo, L1_xattn_bo, L1_xattn_g0, L1_xattn_b0, L1_xattn_g1, L1_xattn_b1, L1_ffn_router_w, L1_ffn_w_gate, L1_ffn_w_up, L1_ffn_w_down):
    import jax
    import jax.numpy as jnp

    def _L0_attn_ref(hidden_states, Wq, bq, Wk, bk, Wv, bv):
        import jax, jax.numpy as jnp
        import numpy as np
        import math
        HEAD_SIZE = 64

        def rotate_every_two(x):
            x1 = x[..., ::2]
            x2 = x[..., 1::2]
            return jnp.stack((-x2, x1), axis=-1).reshape(x.shape)

        def rope_table(seq_len, dtype=jnp.float32):
            pos = jnp.arange(seq_len, dtype=jnp.float32)
            inv = 10000.0 ** (jnp.arange(0, HEAD_SIZE, 2, dtype=jnp.float32) / HEAD_SIZE)
            radians = pos[:, None] / inv
            sincos = jnp.stack((jnp.sin(radians), jnp.cos(radians)), axis=-1).reshape(seq_len, -1)
            t = jnp.repeat(sincos, 2, axis=-1)
            return t.astype(dtype)
        B, S, H = hidden_states.shape
        t = rope_table(S, hidden_states.dtype)
        q = hidden_states @ Wq.T + bq
        k = hidden_states @ Wk.T + bk
        v = hidden_states @ Wv.T + bv
        q = q * t + rotate_every_two(q) * t
        k = k * t + rotate_every_two(k) * t
        scale = math.sqrt(HEAD_SIZE)
        scores = jnp.einsum('bsh,bth->bst', q, k) / scale
        probs = jax.nn.softmax(scores, axis=-1)
        out = jnp.einsum('bst,bth->bsh', probs, v)
        return out

    def _L0_xattn_ref(q, k, v, attention_mask, Wq, bq, Wk, bk, Wv, bv, Wo, bo):
        import jax, jax.numpy as jnp
        import numpy as np
        N_HEADS = 16
        D_MODEL = 128
        HEAD_DIM = D_MODEL // N_HEADS
        MASK_FILL = -100000000.0

        def _split_heads(x):
            B, S, _ = x.shape
            return x.reshape(B, S, N_HEADS, HEAD_DIM).transpose(0, 2, 1, 3)
        qm = _split_heads(q @ Wq.T + bq)
        km = _split_heads(k @ Wk.T + bk)
        vm = _split_heads(v @ Wv.T + bv)
        scores = jnp.einsum('bnlh,bnph->bnlp', qm, km) / np.sqrt(HEAD_DIM).astype(np.float32)
        mask = attention_mask[:, None, None, :]
        scores = jnp.where(mask, scores, MASK_FILL)
        attn = jax.nn.softmax(scores, axis=-1)
        out = jnp.einsum('bnlp,bnph->bnlh', attn, vm)
        B, _, L, _ = out.shape
        out = out.transpose(0, 2, 1, 3).reshape(B, L, D_MODEL)
        return out @ Wo.T + bo

    def _L0_ffn_ref(x, Wq, bq, Wk, bk, Wv, bv, Wo, bo, Wg, bg, W1, b1, W2, b2):
        import jax, jax.numpy as jnp
        import numpy as np
        B, S, H, D, E = (4, 128, 128, 512, 8)
        q = x @ Wq + bq
        k = x @ Wk + bk
        v = x @ Wv + bv
        scale = jnp.asarray(1.0 / np.sqrt(H), x.dtype)
        scores = jnp.einsum('bqh,bkh->bqk', q, k) * scale
        attn = jax.nn.softmax(scores, axis=-1)
        a = jnp.einsum('bqk,bkh->bqh', attn, v) @ Wo + bo
        x = x + a
        gates = jax.nn.softmax(x @ Wg + bg, axis=-1)
        hmid = jax.nn.relu(jnp.einsum('bsh,ehd->bsed', x, W1) + b1)
        eout = jnp.einsum('bsed,edh->bseh', hmid, W2) + b2
        y = jnp.einsum('bse,bseh->bsh', gates, eout)
        return x + y

    def _L1_attn_ref(x, w_qkv, b_qkv, w_out, b_out):
        import jax, jax.numpy as jnp
        import numpy as np
        B, S, D = (2, 256, 128)
        H = 16
        HD = D // H
        WINDOW = 128
        SCALE = HD ** (-0.5)

        def _local_mask(seq_len):
            idx = jnp.arange(seq_len)
            band = jnp.abs(idx[:, None] - idx[None, :]) <= WINDOW // 2
            return jnp.where(band, 0.0, -jnp.inf).astype(jnp.float32)
        b, s, _ = x.shape
        qkv = x @ w_qkv + b_qkv
        qkv = qkv.reshape(b, s, 3, H, HD).transpose(2, 0, 3, 1, 4)
        q, k, v = (qkv[0], qkv[1], qkv[2])
        mask = _local_mask(s)
        scores = jnp.einsum('bhqd,bhkd->bhqk', q, k) * SCALE + mask
        attn = jax.nn.softmax(scores, axis=-1)
        out = jnp.einsum('bhqk,bhkd->bhqd', attn, v)
        out = out.transpose(0, 2, 1, 3).reshape(b, s, D)
        return out @ w_out + b_out

    def _L1_xattn_ref(Q, K, Wq, bq, Wk, bk, Wv, bv, Wo, bo, g0, b0, g1, b1):
        import jax, jax.numpy as jnp
        import numpy as np
        import math
        EPS = 1e-05

        def _layernorm(x, gamma, beta):
            mu = jnp.mean(x, axis=-1, keepdims=True)
            var = jnp.mean(jnp.square(x - mu), axis=-1, keepdims=True)
            return (x - mu) * jax.lax.rsqrt(var + EPS) * gamma + beta
        H = 16
        B, Sq, D = Q.shape
        dh = D // H
        Qp = Q @ Wq + bq
        Kp = K @ Wk + bk
        Vp = Kp @ Wv + bv
        Qh = Qp.reshape(B, Sq, H, dh).transpose(0, 2, 1, 3)
        Kh = Kp.reshape(B, -1, H, dh).transpose(0, 2, 1, 3)
        Vh = Vp.reshape(B, -1, H, dh).transpose(0, 2, 1, 3)
        scores = jnp.einsum('bhqd,bhkd->bhqk', Qh, Kh) / math.sqrt(dh)
        attn = jax.nn.softmax(scores, axis=-1)
        Oh = Qh + jnp.einsum('bhqk,bhkd->bhqd', attn, Vh)
        O = Oh.transpose(0, 2, 1, 3).reshape(B, Sq, D)
        O = _layernorm(O, g0, b0)
        O = O + jax.nn.gelu(O @ Wo + bo, approximate=False)
        O = _layernorm(O, g1, b1)
        return O

    def _L1_ffn_ref(hidden_states, router_w, w_gate, w_up, w_down):
        import jax, jax.numpy as jnp
        import numpy as np
        JITTER_EPS = 0.01
        NEG_INF = -jnp.inf

        def sparsemixer_eval(scores, jitter_eps):
            m1 = jnp.max(scores, axis=-1, keepdims=True)
            ind1 = jnp.argmax(scores, axis=-1)
            factor1 = jnp.maximum(jnp.abs(scores), m1)
            mask1 = jax.lax.stop_gradient((m1 - scores) / factor1 > 2.0 * jitter_eps)
            gates1 = jax.nn.softmax(jnp.where(mask1, NEG_INF, scores), axis=-1)
            mult1 = jnp.take_along_axis(gates1, ind1[:, None], axis=-1)[:, 0]
            E = scores.shape[-1]
            onehot1 = ind1[:, None] == jnp.arange(E)[None, :]
            masked_scores = jnp.where(onehot1, NEG_INF, scores)
            m2 = jnp.max(masked_scores, axis=-1, keepdims=True)
            ind2 = jnp.argmax(masked_scores, axis=-1)
            factor2 = jnp.maximum(jnp.abs(scores), m2)
            mask2 = jax.lax.stop_gradient((m2 - scores) / factor2 > 2.0 * jitter_eps)
            gates2 = jax.nn.softmax(jnp.where(mask2, NEG_INF, masked_scores), axis=-1)
            mult2 = jnp.take_along_axis(gates2, ind2[:, None], axis=-1)[:, 0]
            multiplier = jnp.stack([mult1, mult2], axis=-1)
            selected = jnp.stack([ind1, ind2], axis=-1)
            return (multiplier, selected)
        B, S, H = hidden_states.shape
        E = router_w.shape[0]
        x = hidden_states.reshape(-1, H)
        T = x.shape[0]
        logits = x @ router_w.T
        routing_weights, selected = sparsemixer_eval(logits, JITTER_EPS)
        tok = jnp.arange(T)
        dense_w = jnp.zeros((T, E), dtype=x.dtype)
        dense_w = dense_w.at[tok, selected[:, 0]].add(routing_weights[:, 0])
        dense_w = dense_w.at[tok, selected[:, 1]].add(routing_weights[:, 1])
        out = jnp.zeros_like(x)
        for e in range(E):
            h = jax.nn.silu(x @ w_gate[e].T) * (x @ w_up[e].T)
            out = out + dense_w[:, e:e + 1] * (h @ w_down[e].T)
        return out.reshape(B, S, H)
    x = _layernorm(x + _L0_attn_ref(x, L0_attn_Wq, L0_attn_bq, L0_attn_Wk, L0_attn_bk, L0_attn_Wv, L0_attn_bv), axis=-1)
    x = _layernorm(x + _L0_xattn_ref(x, ctx_1024, ctx_1024, mask_BxS2_bf1, L0_xattn_Wq, L0_xattn_bq, L0_xattn_Wk, L0_xattn_bk, L0_xattn_Wv, L0_xattn_bv, L0_xattn_Wo, L0_xattn_bo), axis=-1)
    x = _layernorm(x + _L0_ffn_ref(x, L0_ffn_Wq, L0_ffn_bq, L0_ffn_Wk, L0_ffn_bk, L0_ffn_Wv, L0_ffn_bv, L0_ffn_Wo, L0_ffn_bo, L0_ffn_Wg, L0_ffn_bg, L0_ffn_W1, L0_ffn_b1, L0_ffn_W2, L0_ffn_b2), axis=-1)
    x = _layernorm(x + _L1_attn_ref(x, L1_attn_w_qkv, L1_attn_b_qkv, L1_attn_w_out, L1_attn_b_out), axis=-1)
    x = _layernorm(x + _L1_xattn_ref(x, ctx_1024, L1_xattn_Wq, L1_xattn_bq, L1_xattn_Wk, L1_xattn_bk, L1_xattn_Wv, L1_xattn_bv, L1_xattn_Wo, L1_xattn_bo, L1_xattn_g0, L1_xattn_b0, L1_xattn_g1, L1_xattn_b1), axis=-1)
    x = _layernorm(x + _L1_ffn_ref(x, L1_ffn_router_w, L1_ffn_w_gate, L1_ffn_w_up, L1_ffn_w_down), axis=-1)
    return x

_drawn_inputs = setup_inputs


def setup_inputs(seed=0):
    import zlib

    import numpy as np

    out = dict(_drawn_inputs(seed))
    spreads = {'L0_xattn_bq': (0.0, 0.307),
     'L0_xattn_bk': (0.0, 0.8),
     'L0_xattn_bv': (0.0, 0.1),
     'L0_xattn_bo': (0.0, 0.1),
     'L0_ffn_bq': (0.0, 0.8),
     'L0_ffn_bk': (0.0, 0.8),
     'L0_ffn_bv': (0.0, 0.1),
     'L0_ffn_bo': (0.0, 0.1),
     'L0_ffn_bg': (0.0, 0.799),
     'L0_ffn_b1': (0.0, 0.469),
     'L0_ffn_b2': (0.0, 0.301),
     'L1_xattn_bq': (0.0, 0.1),
     'L1_xattn_bk': (0.0, 0.1),
     'L1_xattn_bv': (0.0, 0.1),
     'L1_xattn_bo': (0.0, 0.1),
     'L1_xattn_g0': (1.0, 0.2),
     'L1_xattn_b0': (0.0, 0.1),
     'L1_xattn_g1': (1.0, 0.2),
     'L1_xattn_b1': (0.0, 0.1)}
    factors = {'L0_attn_bk': 3.68,
     'L1_attn_b_qkv': 2.981,
     'L1_attn_b_out': 3.262,
     'L1_ffn_router_w': 5.622,
     'L1_ffn_w_gate': 4.94,
     'L1_ffn_w_up': 4.908,
     'L1_ffn_w_down': 4.931}
    for name, (base, spread) in spreads.items():
        noise = np.random.default_rng([zlib.crc32(name.encode()), seed]).standard_normal(out[name].shape)
        drawn = base * np.exp(spread * noise) if base else spread * noise
        out[name] = jnp.asarray(drawn.astype(out[name].dtype))
    for name, factor in factors.items():
        out[name] = (out[name] * factor).astype(out[name].dtype)
    return out
```

```python
from contextlib import ExitStack

import concourse.bass as bass
from concourse import mybir

F32 = mybir.dt.float32
F16 = mybir.dt.float16
BF16 = mybir.dt.bfloat16
U8 = mybir.dt.uint8
ALU = mybir.AluOpType
ACT = mybir.ActivationFunctionType
AX = mybir.AxisListType.X

P = 128
D = 128
SEQ = 64
BATCH = 32
TOKENS = BATCH * SEQ
CHUNK = 512
TILES = CHUNK // P
SEQS = CHUNK // SEQ
SLOTS = 2
ITERS = TOKENS // (CHUNK * SLOTS)
HEADS = 16
HD = D // HEADS
PAIRS = HEADS // 2
GROUPS = 4
E = 8
D0 = 512 // P
F1 = 256 // P
BANKS = 6
VRING = 3
RING = 4
VSTEP = 188
VBACK = 60
VW = 32 + PAIRS * (VSTEP + 1)
EPS = 1e-5
MHA_SCALE = float(HD) ** -0.5
ONE_SCALE = (0.125, float(D) ** -0.5)
MASKED = -1e8
LINKS = 152

W_ONE = {(0, "q"): 0, (0, "k"): 1, (0, "v"): 2, (1, "q"): 3, (1, "k"): 4, (1, "v"): 5, (1, "o"): 6}
W_MHA = {(m, w): 7 + 4 * m + n for m in range(3) for n, w in enumerate("qkvo")}
NPROJ = 19
W_G0 = NPROJ * D
W_G1 = W_G0 + E
W_UP0 = W_G1 + E
W_DN0 = W_UP0 + E * D0 * D
W_GA1 = W_DN0 + E * D0 * D
W_UP1 = W_GA1 + E * F1 * D
W_DN1 = W_UP1 + E * F1 * D
NW = W_DN1 + E * F1 * D
R_ONE = {(0, "v"): 0, (1, "v"): 1, (1, "o"): 2}
R_MHA = {(m, w): 3 + 2 * m + n for m in range(3) for n, w in enumerate("vo")}
R_G0 = 9 * D
R_B2 = R_G0 + E
NR = R_B2 + D
C_ONE = {(0, "q"): 0, (0, "k"): 1, (1, "q"): 2, (1, "k"): 3}
C_MHA = {(m, w): 4 + 2 * m + n for m in range(3) for n, w in enumerate("qk")}
C_B1 = 10
C_PART = C_B1 + E * D0
NC = C_PART + 2
K_ID, K_PERM, K_CROSS, K_ROPE, K_SIGN = 0, 128, 256, 384, 448
K_IOTA = K_SIGN + 1
K_LN = K_IOTA + E
NK = K_LN + 4 * D
S_SEL, S_ONES, NS = 0, PAIRS * D, PAIRS * D + D


def row_of(h, i):
    p, j = h % 2, h // 2
    return 64 * (j // 4) + 32 * p + 4 * i + j % 4


def vcol_of(h, i):
    return 64 * (h % 2) + 8 * (h // 2) + i


def schedule():
    def tr(name):
        for s in range(SLOTS):
            yield ("bank", ("T", name, s))
            yield ("split", ("T", name, s))

    def single(a):
        for s in range(SLOTS):
            for w in "qkv":
                yield ("bank", (w, a, s))
            yield ("split", ("v", a, s))
            yield ("split", ("q", a, s))
            yield ("split", ("k", a, s))
        for s in range(SLOTS):
            yield ("bank", ("s", a, s))
        for s in range(SLOTS):
            yield ("split", ("p", a, s))
            yield ("bank", ("pt", a, s))
        for s in range(SLOTS):
            yield ("bank", ("o", a, s))
            if a:
                yield ("split", ("o", a, s))
        if a:
            for s in range(SLOTS):
                yield ("bank", ("wo", a, s))

    def mha(m):
        for s in range(SLOTS):
            yield ("bank", ("mk", m, s))
            yield ("split", ("mk", m, s))
            yield ("bank", ("mq", m, s))
            yield ("split", ("mq", m, s))
        n = SLOTS * TILES
        for i in range(VRING):
            yield ("bank", ("mv", m, i))
        for i in range(n + 3):
            if i < n:
                yield ("bank", ("n", m, i, 0))
                yield ("bank", ("n", m, i, 1))
            if 1 <= i <= n:
                yield ("bank", ("mt", m, i - 1))
            if 2 <= i < n + 2:
                for b in range(2):
                    yield ("bank", ("t", m, i - 2, b))
                    yield ("ring", ("t", m, i - 2, b))
            if i >= 3:
                if (i - 3) % 2 == 0:
                    yield ("acc", ("pv", m, (i - 3) // 2))
                if i - 3 + VRING < n:
                    yield ("bank", ("mv", m, i - 3 + VRING))
        for s in range(SLOTS):
            if m < 2:
                yield ("split", ("mo", m, s))
                yield ("bank", ("mw", m, s))
            else:
                yield ("bank", ("ot", s))
        if m == 2:
            yield from tr("o")
            for s in range(SLOTS):
                yield ("bank", ("mw", m, s))

    def ffn(f):
        for s in range(SLOTS):
            yield ("bank", ("g", f, s))
        if f == 0:
            for s in range(SLOTS):
                yield ("bank", ("gt", s))
                yield ("bank", ("gb", s))
        inner = (D0, F1)[f]
        n = SLOTS * E * inner
        for i in range(n + FLAG):
            if i < n:
                yield ("bank", ("up", f, i))
                if f == 1:
                    yield ("bank", ("ga", f, i))
                yield ("ring", ("h", f, i))
            if i >= FLAG and (i - FLAG) % inner == 0:
                yield ("acc", ("y", f, (i - FLAG) // inner))

    yield from tr("c")
    yield from tr("x0")
    yield from single(0)
    yield from tr("x1")
    yield from mha(0)
    yield from tr("x2")
    yield from single(1)
    yield from tr("x3")
    yield from ffn(0)
    yield from tr("x4")
    yield from mha(1)
    yield from tr("x5")
    yield from mha(2)
    yield from tr("x6")
    yield from ffn(1)


FLAG = 3


class Signal:

    def __init__(self, sem, steps, inc=1, base=0):
        self.sem, self.steps, self.inc, self.base = sem, list(steps), inc, base
        self.at = {x: n for n, x in enumerate(self.steps)}

    def after(self, it, step):
        return it * (len(self.steps) * self.inc) + (self.base + (self.at[step] + 1) * self.inc)

    def before(self, it, step):
        return it * (len(self.steps) * self.inc) + (self.base + self.at[step] * self.inc)


def build(nc, t):
    plan = list(schedule())
    banks = [x for k, x in plan if k == "bank"]
    accs = [x for k, x in plan if k == "acc"]
    splits = [x for k, x in plan if k == "split"]
    rings = [x for k, x in plan if k == "ring"]
    bank_at = {x: n for n, x in enumerate(banks)}
    acc_at = {x: n for n, x in enumerate(accs)}
    ring_at = {x: n for n, x in enumerate(rings)}
    n_tiles = SLOTS * TILES
    lns = ["l0", "l1", "l2", "l3", "la", "lb", "l4", "l5"]
    links = [0]

    ctx = ExitStack()
    with ctx:
        def sb(name, shape, dt):
            return ctx.enter_context(nc.sbuf_tensor(name, shape, dt))

        def sem(name):
            return ctx.enter_context(nc.semaphore(name))

        w = sb("w", [P, 2, NW], F16)
        rb = sb("rb", [P, R_B2], F16)
        b2 = sb("b2", [P, D], F16)
        cb = sb("cb", [P, NC], F32)
        kc = sb("kc", [P, NK], F32)
        ident16 = sb("ident16", [P, P], F16)
        identb = sb("identb", [P, P], BF16)
        negsel = sb("negsel", [P, PAIRS, P], BF16)
        ones_rows = sb("ones_rows", [P, P], F16)
        half = sb("half", [P, TILES], F32)
        mk_bias = sb("mk_bias", [P, SLOTS, SEQS], F32)
        mk8 = sb("mk8", [P, SLOTS, SEQS], U8)
        seq_any = sb("seq_any", [P, SLOTS, SEQS], F32)
        xs = sb("xs", [P, SLOTS, TILES, D], F32)
        ys = sb("ys", [P, SLOTS, TILES, D], F32)
        os_ = ys[:].rearrange("p s t d -> p s (t d)")
        zs = sb("zs", [P, SLOTS, TILES, D], F32)
        qs = zs[:].rearrange("p s t d -> p s (t d)")
        xt = sb("xt", [P, SLOTS, 2, CHUNK], F16)
        ct = sb("ct", [P, SLOTS, 2, CHUNK], F16)
        qh = sb("qh", [P, SLOTS, 2, CHUNK], F16)
        kh = sb("kh", [P, SLOTS, 2, CHUNK], F16)
        oh = kh
        qstack = sb("qstack", [P, SLOTS, GROUPS, CHUNK], F16)
        kstack = sb("kstack", [P, SLOTS, 2, GROUPS * SEQS, 2, SEQ], F16)
        vm = sb("vm", [P, VRING, 2, 2, VW], F16)
        r32 = sb("r32", [P, RING, CHUNK], F32)
        rhl = sb("rhl", [P, RING, 2, CHUNK], F16)
        rden = sb("rden", [P, 2, 256], F32)
        mx = sb("mx", [P, SLOTS, TILES, HEADS], F32)
        mhl = sb("mhl", [P, 2, P], BF16)
        mt = sb("mt", [P, 2, P], BF16)
        amask = sb("amask", [P, SLOTS, CHUNK], BF16)
        kmask8 = sb("kmask8", [P, SLOTS, CHUNK], U8)
        stats = sb("stats", [P, SLOTS, TILES, 6], F32)
        mv = sb("mv", [P, SLOTS, TILES, 2], F32)
        ve = sb("ve", [P, SLOTS, TILES], F32)
        rstd = sb("rstd", [P, SLOTS, TILES], F32)
        sm = sb("sm", [P, SLOTS, 4, TILES], F32)
        gates = sb("gates", [P, SLOTS, TILES, E], F32)
        gw = sb("gw", [P, SLOTS, 12, TILES, E], F32)
        gm = sb("gm", [P, SLOTS, 8, TILES], F32)
        gstack = qstack[:, :, 0].rearrange("p s (t c) -> p s t c", t=TILES)
        gtr = qh[:, :, 0]
        bank = [ctx.enter_context(nc.psum_tensor(f"bank{i}", [P, CHUNK], F32)) for i in range(BANKS)]
        acc = [ctx.enter_context(nc.psum_tensor(f"acc{i}", [P, CHUNK], F32)) for i in range(2)]
        kd = [nc.dram_tensor(f"k_scratch{s}", [P, GROUPS, CHUNK], F16, kind="Internal").ap() for s in range(SLOTS)]
        qd = [nc.dram_tensor(f"q_scratch{s}", [P, GROUPS, CHUNK], F16, kind="Internal").ap() for s in range(SLOTS)]

        stage = [kstack[:, s].rearrange("p v g u t -> p (v g u t)").bitcast(F32) for s in range(SLOTS)]
        SW = GROUPS * 4 * CHUNK // 2
        pieces = [(o, min(SW, NW - o)) for o in range(0, NW, SW)]

        consts_in = sem("consts_in")
        stage_in = [sem(f"stage_in{i}") for i in range(2)]
        rot_done, w_hi, w_lo = sem("rot_done"), sem("w_hi"), sem("w_lo")
        small_prep, pool_prep = sem("small_prep"), sem("pool_prep")
        dve_link = sem("dve_link")
        pool_cleared = sem("pool_cleared")
        aggr_turn = sem("aggr_turn")
        prep_link = sem("prep_link")
        pairs = lambda xs_: [(x, s) for x in xs_ for s in range(SLOTS)]
        chunk_in = [Signal(sem(f"chunk_in{s}"), ["in"], 64) for s in range(SLOTS)]
        stored = Signal(sem("stored"), range(SLOTS), 16, base=1)
        full = [Signal(sem(f"bank_full{b}"), banks[b::BANKS]) for b in range(BANKS)]
        read = [Signal(sem(f"bank_read{b}"), banks[b::BANKS], base=1) for b in range(BANKS)]
        acc_full = [Signal(sem(f"acc_full{b}"), accs[b::2]) for b in range(2)]
        acc_read = [Signal(sem(f"acc_read{b}"), accs[b::2], base=1) for b in range(2)]
        hi = Signal(sem("split_hi"), splits)
        from_sbuf = [x for x in splits if x[0] in ("p", "mo") or x[:2] in (("q", 0), ("k", 0), ("mk", 0))]
        lo = Signal(sem("split_lo"), from_sbuf)
        hidden = [r for r in rings if r[0] == "h"]
        r_hi = Signal(sem("ring_hi"), hidden)
        r_lo = Signal(sem("ring_lo"), rings)
        ends = {r: (("pv", r[1], r[2] // 2) if r[0] == "t" else ("y", r[1], r[2] // (D0, F1)[r[1]])) for r in rings
                if (r[0] == "t" and r[2] % 2 and r[3]) or (r[0] == "h" and (r[2] + 1) % (D0, F1)[r[1]] == 0)}
        r_used = Signal(sem("ring_used"), [r for r in rings if r not in ends])
        f32_ready = Signal(sem("f32_ready"), [(w_, 0, s) for s in range(SLOTS) for w_ in "qk"]
                           + [(k, m, s) for k, m in (("p", 0), ("mk", 0), ("mo", 0), ("p", 1), ("mo", 1), ("mo", 2)) for s in range(SLOTS)])
        smax = Signal(sem("softmax_max"), pairs(range(2)))
        sexp = Signal(sem("softmax_exp"), pairs(range(2)))
        kq_stored = {x: [Signal(sem(f"{x}_stored{s}"), range(3), 64) for s in range(SLOTS)] for x in "kq"}
        k_in = [Signal(sem(f"k_stacked{s}"), range(3), 64) for s in range(SLOTS)]
        q_in = [Signal(sem(f"q_stacked{s}"), range(3), 16) for s in range(SLOTS)]
        halves3 = [(m, h) for m in range(3) for h in range(n_tiles // 2)]
        max_split = Signal(sem("max_split"), [(m, i) for m in range(3) for i in range(n_tiles)])
        v_hi = Signal(sem("v_hi"), [(m, i) for m in range(3) for i in range(n_tiles)])
        den_ln = Signal(sem("den_ln"), halves3)
        den_done = Signal(sem("den_reciprocal"), halves3)
        variance = Signal(sem("variance"), pairs(lns))
        rstd_done = Signal(sem("rstd"), pairs(lns))
        normed = Signal(sem("normalised"), pairs(lns[:2] + ["x1"] + lns[2:]))
        masks_ready = Signal(sem("masks_ready"), range(SLOTS))
        gate_in = Signal(sem("gate_shifted"), pairs(range(2)))
        gate_exp = Signal(sem("gate_exp"), pairs(range(2)))
        gate_stack = Signal(sem("gate_stack"), range(SLOTS))

        block = ctx.enter_context(nc.Block())

        def full_of(name):
            return full[bank_at[name] % BANKS] if name in bank_at else acc_full[acc_at[name] % 2]

        def read_of(name):
            return read[bank_at[name] % BANKS] if name in bank_at else acc_read[acc_at[name] % 2]

        def full_sem(name):
            return full_of(name).sem

        def full_value(it, name):
            return full_of(name).after(it, name)

        def read_sem(name):
            return read_of(name).sem

        def read_value(it, name):
            return read_of(name).after(it, name)

        def free_sem(name):
            return read_of(name).sem

        def free_value(it, name):
            return read_of(name).before(it, name)

        def split_sem(name):
            return lo.sem if name in lo.at else read_sem(name)

        def split_value(it, name):
            return lo.after(it, name) if name in lo.at else read_value(it, name)

        def used_sem(ri):
            r = rings[ri]
            return full_sem(ends[r]) if r in ends else r_used.sem

        def used_value(it, ri):
            r = rings[ri]
            return full_value(it, ends[r]) if r in ends else r_used.after(it, r)

        def link_value(it):
            links[0] += 1
            return it * LINKS + links[0]

        def bank_of(name):
            return bank[bank_at[name] % BANKS] if name in bank_at else acc[acc_at[name] % 2]

        def flat(buf, s):
            return buf[:, s].rearrange("p t d -> p (t d)")

        def tiled(ap, n=TILES):
            return ap.rearrange("p (t d) -> p t d", t=n)

        def spread(ap, n):
            return ap.unsqueeze(2).broadcast_to([ap.shape[0], ap.shape[1], n])

        def repeat(ap, n):
            return ap.unsqueeze(1).broadcast_to([ap.shape[0], n, ap.shape[1]])

        def v_dst(i, k, p):
            return vm[64 * p:64 * p + 64, i % VRING, k, :, 32 * p:32 * p + PAIRS * (VSTEP + 1)].rearrange(
                "q s (j w) -> q s j w", j=PAIRS)[:, :, :, 0:4 * HD:4]

        def v_src(name, p):
            return bank_of(name)[64 * p:64 * p + 64, 0:128].rearrange("q (s j i) -> q s j i", s=2, i=HD)

        single_dst = {"v": qstack, "q": qh, "k": kh, "p": kh, "o": oh}

        @block.sync
        def _(sp):
            zf = zs[:].rearrange("p s t d -> p (s t d)")
            yf = ys[:].rearrange("p s t d -> p (s t d)")
            sp.dma_start(kc[:], t["consts"]).then_inc(consts_in, 16)
            sp.dma_start(cb[:], t["col_bias"]).then_inc(consts_in, 16)
            sp.dma_start(r32[:].rearrange("p r c -> p (r c)")[:, 0:NS], t["consts16"]).then_inc(consts_in, 16)
            sp.dma_start(yf[:, 0:1024], t["row_bias"][:, 0:1024]).then_inc(consts_in, 16)
            sp.dma_start(zf[:, 0:NR - 1024], t["row_bias"][:, 1024:NR]).then_inc(consts_in, 16)
            for n, (o, c) in enumerate(pieces):
                if n >= 2:
                    sp.wait_ge(w_lo, n - 1)
                sp.dma_start(stage[n % 2][:, 0:c], t["weights"][:, o:o + c]).then_inc(stage_in[n % 2], 16)
            sp.sem_inc(stored.sem, 1)
            sp.wait_ge(small_prep, 1)
            with sp.Fori(0, ITERS) as it:
                sp.wait_ge(stored.sem, stored.before(it, 0))
                for s in range(SLOTS):
                    base = it * (SLOTS * CHUNK) + s * CHUNK
                    sp.dma_start(xs[:, s], t["x"][bass.ds(base, CHUNK), :].rearrange("(t p) d -> p t d", p=P)).then_inc(chunk_in[s].sem, 16)
                    sp.dma_start(zs[:, s], t["ctx"][bass.ds(base, CHUNK), :].rearrange("(t p) d -> p t d", p=P)).then_inc(chunk_in[s].sem, 16)
                    sp.dma_start(kmask8[:, s], t["mask_row"][:, bass.ds(base, CHUNK)].broadcast_to([P, CHUNK])).then_inc(chunk_in[s].sem, 16)
                    sp.dma_start(mk8[:, s], t["mask_cols"][:, bass.ds(it * (SLOTS * SEQS) + s * SEQS, SEQS)]).then_inc(chunk_in[s].sem, 16)
                for m in range(3):
                    for s in range(SLOTS):
                        for x, src, dst in (("k", kh, kd), ("q", qh, qd)):
                            sp.wait_ge(split_sem(("m" + x, m, s)), split_value(it, ("m" + x, m, s)))
                            view = dst[s].rearrange("(ui a b) g t -> a b ui g t", a=2, b=2)
                            for a in range(2):
                                for b in range(2):
                                    sp.dma_start(view[a, b], src[:, s, a if x == "k" else b]).then_inc(kq_stored[x][s].sem, 16)
                        sp.wait_ge(kq_stored["k"][s].sem, kq_stored["k"][s].after(it, m))
                        for u in range(4):
                            sp.dma_start(kstack[32 * u:32 * u + 32, s, u // 2, :, u % 2, :], kd[s][32 * u:32 * u + 32].rearrange("r g (s k) -> r (g s) k", k=SEQ)).then_inc(k_in[s].sem, 16)
                        sp.wait_ge(kq_stored["q"][s].sem, kq_stored["q"][s].after(it, m))
                        sp.dma_start(qstack[:, s], qd[s]).then_inc(q_in[s].sem, 16)
                for s in range(SLOTS):
                    base = it * (SLOTS * CHUNK) + s * CHUNK
                    sp.wait_ge(normed.sem, normed.after(it, ("l5", s)))
                    sp.dma_start(t["out"][bass.ds(base, CHUNK), :].rearrange("(t p) d -> p t d", p=P), xs[:, s]).then_inc(stored.sem, 16)
            sp.wait_ge(stored.sem, stored.before(ITERS, 0))

        @block.tensor
        def _(pe):
            mm = nc.tensor.matmul

            def prod3(out, left, right, first=True, last=True, check=False):
                mm(out, left(0), right(0), start=first, stop=False, skip_group_check=check)
                mm(out, left(0), right(1), start=False, stop=False, skip_group_check=check)
                return mm(out, left(1), right(0), start=False, stop=last, skip_group_check=check)

            def weight(col, n=D):
                return lambda k: w[:, k, col:col + n]

            def cols(buf, s, a, n):
                return lambda k: buf[:, s, k, a:a + n]

            def transposed(it, name, src, eye=K_ID):
                pe.wait_ge(free_sem(name), free_value(it, name))
                o = bank_of(name)
                for i in range(TILES):
                    last = nc.tensor.transpose(o[:, i * P:(i + 1) * P], src[:, i, :], kc[:, eye:eye + P])
                last.then_inc(full_sem(name), 1)

            def token_major(it, name, src, s, col, bias, n=D):
                pe.wait_ge(free_sem(name), free_value(it, name))
                o = bank_of(name)
                for i in range(TILES):
                    out = o[:, i * n:(i + 1) * n]
                    last = prod3(out, cols(src, s, i * P, P), weight(col, n), last=bias is None)
                    if bias is not None:
                        last = mm(out, ones_rows[:], rb[:, bias:bias + n], start=False, stop=True)
                last.then_inc(full_sem(name), 1)

            def feature_major(it, name, col, src, s):
                pe.wait_ge(free_sem(name), free_value(it, name))
                prod3(bank_of(name)[:], weight(col), lambda k: src[:, s, k]).then_inc(full_sem(name), 1)

            def single(it, a, tname):
                for s in range(SLOTS):
                    pe.wait_ge(split_sem(("T", tname, s)), split_value(it, ("T", tname, s)))
                    for x in "qk":
                        feature_major(it, (x, a, s), W_ONE[a, x] * D, xt, s)
                    token_major(it, ("v", a, s), xt, s, W_ONE[a, "v"] * D, R_ONE[a, "v"] * D)
                for s in range(SLOTS):
                    pe.wait_ge(split_sem(("k", a, s)), split_value(it, ("k", a, s)))
                    pe.wait_ge(free_sem(("s", a, s)), free_value(it, ("s", a, s)))
                    o = bank_of(("s", a, s))
                    for i in range(TILES):
                        last = prod3(o[:, i * P:(i + 1) * P], cols(qh, s, i * P, P), cols(kh, s, i * P, P))
                    last.then_inc(full_sem(("s", a, s)), 1)
                for s in range(SLOTS):
                    pe.wait_ge(split_sem(("p", a, s)), split_value(it, ("p", a, s)))
                    pe.wait_ge(free_sem(("pt", a, s)), free_value(it, ("pt", a, s)))
                    o = bank_of(("pt", a, s))[:].bitcast(F16)
                    for k in range(2):
                        for i in range(TILES):
                            c = k * CHUNK + i * P
                            last = nc.tensor.transpose(o[:, c:c + P], kh[:, s, k, i * P:(i + 1) * P], ident16[:])
                    last.then_inc(full_sem(("pt", a, s)), 1)
                for s in range(SLOTS):
                    pe.wait_ge(read_sem(("pt", a, s)), read_value(it, ("pt", a, s)))
                    pe.wait_ge(free_sem(("o", a, s)), free_value(it, ("o", a, s)))
                    o = bank_of(("o", a, s))
                    for i in range(TILES):
                        v, pt = cols(qstack, s, i * P, P), cols(qh, s, i * P, P)
                        last = prod3(o[:, i * P:(i + 1) * P], *((v, pt) if a else (pt, v)))
                    last.then_inc(full_sem(("o", a, s)), 1)
                if a:
                    for s in range(SLOTS):
                        pe.wait_ge(split_sem(("o", a, s)), split_value(it, ("o", a, s)))
                        token_major(it, ("wo", a, s), oh, s, W_ONE[a, "o"] * D, R_ONE[a, "o"] * D)

            def mha(it, m, tname):
                src_kv = xt if m == 1 else ct
                for s in range(SLOTS):
                    pe.wait_ge(split_sem(("T", tname, s)), split_value(it, ("T", tname, s)))
                    feature_major(it, ("mk", m, s), W_MHA[m, "k"] * D, src_kv, s)
                    feature_major(it, ("mq", m, s), W_MHA[m, "q"] * D, xt, s)

                def values_of(i):
                    s = i // TILES
                    src = kh if m == 2 else src_kv
                    if m == 2:
                        pe.wait_ge(split_sem(("mk", m, s)), split_value(it, ("mk", m, s)))
                    pe.wait_ge(free_sem(("mv", m, i)), free_value(it, ("mv", m, i)))
                    o = bank_of(("mv", m, i))
                    for b in range(2):
                        a0 = (i % TILES) * P + b * SEQ
                        for p in range(2):
                            out = o[64 * p:64 * p + 64, b * 64:(b + 1) * 64]
                            prod3(out, cols(src, s, a0, SEQ), weight(W_MHA[m, "v"] * D + 64 * p, 64), last=False)
                            c = R_MHA[m, "v"] * D + 64 * p
                            last = mm(out, ones_rows[:, 0:SEQ], rb[:, c:c + 64], start=False, stop=True)
                    last.then_inc(full_sem(("mv", m, i)), 1)

                def scores(i):
                    s = i // TILES
                    if i % TILES == 0:
                        pe.wait_ge(k_in[s].sem, k_in[s].after(it, m))
                        pe.wait_ge(q_in[s].sem, q_in[s].after(it, m))
                        if m == 0:
                            pe.wait_ge(masks_ready.sem, masks_ready.after(it, s))
                    for hb in range(2):
                        pe.wait_ge(free_sem(("n", m, i, hb)), free_value(it, ("n", m, i, hb)))
                        o = bank_of(("n", m, i, hb))
                        for gi in range(2):
                            for b in range(2):
                                c0 = (i % TILES) * P + b * SEQ
                                g = 2 * hb + gi
                                keys = kstack[:, s, :, g * SEQS + c0 // SEQ].rearrange("p v u k -> p v (u k)")
                                out = o[b * SEQ:(b + 1) * SEQ, gi * 256:(gi + 1) * 256]
                                last = mm(out, qstack[:, s, g, c0:c0 + SEQ], keys, start=True, stop=m > 0)
                                if m == 0:
                                    last = mm(out, ones_rows[:, 0:SEQ], repeat(amask[:, s, c0:c0 + SEQ], 4), start=False, stop=True)
                        last.then_inc(full_sem(("n", m, i, hb)), 1)

                def maxima_t(i):
                    pe.wait_ge(max_split.sem, max_split.after(it, (m, i)))
                    pe.wait_ge(free_sem(("mt", m, i)), free_value(it, ("mt", m, i)))
                    o = bank_of(("mt", m, i))[:].bitcast(BF16)
                    nc.tensor.transpose(o[:, 0:P], mhl[:, i % 2, :], identb[:]).then_inc(full_sem(("mt", m, i)), 1)

                def scores_t(i):
                    s = i // TILES
                    pe.wait_ge(read_sem(("mt", m, i)), read_value(it, ("mt", m, i)))
                    for b in range(2):
                        c0 = (i % TILES) * P + b * SEQ
                        pe.wait_ge(free_sem(("t", m, i, b)), free_value(it, ("t", m, i, b)))
                        o = bank_of(("t", m, i, b))
                        for j in range(PAIRS):
                            vp, g = j // 4, j % 4
                            out = o[:, j * SEQ:(j + 1) * SEQ]
                            mm(out, kstack[:, s, vp, g * SEQS + c0 // SEQ].rearrange("p u k -> p (u k)"), qstack[:, s, g, c0:c0 + SEQ], start=True, stop=False)
                            last = mm(out, negsel[:, j, :], mt[:, i % 2, b * SEQ:(b + 1) * SEQ], start=False, stop=True)
                        last.then_inc(full_sem(("t", m, i, b)), 1)

                def attend(i):
                    h = i // 2
                    name = ("pv", m, h)
                    if i % 2 == 0:
                        pe.wait_ge(free_sem(name), free_value(it, name))
                    pe.wait_ge(read_sem(("mv", m, i)), read_value(it, ("mv", m, i)))
                    o = bank_of(name)
                    for b in range(2):
                        r = ("t", m, i, b)
                        pe.wait_ge(r_lo.sem, r_lo.after(it, r))
                        ri = ring_at[r] % RING
                        sq = 2 * (i % 2) + b
                        for vp in range(2):
                            out = o[:, vp * 256 + sq * SEQ:vp * 256 + (sq + 1) * SEQ]
                            for g in range(4):
                                j = 4 * vp + g
                                c = VSTEP * j - VBACK * vp
                                last = prod3(out, lambda k: vm[:, i % VRING, k, b, c:c + P],
                                             lambda k: rhl[:, ri, k, j * SEQ:(j + 1) * SEQ], first=g == 0, last=g == 3)
                        if b == 0:
                            last.then_inc(r_used.sem, 1)
                    if i % 2 == 1:
                        last.then_inc(full_sem(name), 1)
                    else:
                        last.then_inc(r_used.sem, 1)

                for i in range(VRING):
                    values_of(i)
                for i in range(n_tiles + 3):
                    if i < n_tiles:
                        scores(i)
                    if 1 <= i <= n_tiles:
                        maxima_t(i - 1)
                    if 2 <= i < n_tiles + 2:
                        scores_t(i - 2)
                    if i >= 3:
                        attend(i - 3)
                        if i - 3 + VRING < n_tiles:
                            values_of(i - 3 + VRING)
                if m == 2:
                    for s in range(SLOTS):
                        pe.wait_ge(f32_ready.sem, f32_ready.after(it, ("mo", m, s)))
                        transposed(it, ("ot", s), tiled(os_[:, s]), K_PERM)
                    for s in range(SLOTS):
                        pe.wait_ge(normed.sem, normed.after(it, ("la", s)))
                        transposed(it, ("T", "o", s), zs[:, s])
                for s in range(SLOTS):
                    pe.wait_ge(split_sem(("T", "o", s) if m == 2 else ("mo", m, s)), split_value(it, ("T", "o", s) if m == 2 else ("mo", m, s)))
                    token_major(it, ("mw", m, s), xt if m == 2 else oh, s, W_MHA[m, "o"] * D, R_MHA[m, "o"] * D)

            def ffn(it, f, tname):
                for s in range(SLOTS):
                    pe.wait_ge(split_sem(("T", tname, s)), split_value(it, ("T", tname, s)))
                    token_major(it, ("g", f, s), xt, s, W_G1 if f else W_G0, None if f else R_G0, E)
                if f == 0:
                    for s in range(SLOTS):
                        pe.wait_ge(gate_stack.sem, gate_stack.after(it, s))
                        pe.wait_ge(free_sem(("gt", s)), free_value(it, ("gt", s)))
                        o = bank_of(("gt", s))[:].bitcast(F16)
                        for i in range(TILES):
                            last = nc.tensor.transpose(o[:, i * P:(i + 1) * P], gstack[:, s, i, :], ident16[:])
                        last.then_inc(full_sem(("gt", s)), 1)
                        pe.wait_ge(read_sem(("gt", s)), read_value(it, ("gt", s)))
                        pe.wait_ge(free_sem(("gb", s)), free_value(it, ("gb", s)))
                        o = bank_of(("gb", s))
                        for i in range(TILES):
                            last = mm(o[:, i * P:(i + 1) * P], gtr[:, s, i * P:(i + 1) * P], b2[:], start=True, stop=True)
                        last.then_inc(full_sem(("gb", s)), 1)
                inner = (D0, F1)[f]
                n = SLOTS * E * inner
                up, down = (W_UP0, W_UP1)[f], (W_DN0, W_DN1)[f]
                for i in range(n + FLAG):
                    if i < n:
                        s, c = i // (E * inner), i % (E * inner)
                        if f == 1:
                            feature_major(it, ("ga", f, i), W_GA1 + c * D, xt, s)
                        feature_major(it, ("up", f, i), up + c * D, xt, s)
                    if i >= FLAG:
                        q = i - FLAG
                        c = q % (E * inner)
                        name = ("y", f, q // inner)
                        if q % inner == 0:
                            pe.wait_ge(free_sem(name), free_value(it, name))
                        o = bank_of(name)
                        pe.wait_ge(r_lo.sem, r_lo.after(it, ("h", f, q)))
                        ri = ring_at["h", f, q] % RING
                        for ti in range(TILES):
                            last = prod3(o[:, ti * P:(ti + 1) * P], lambda k: rhl[:, ri, k, ti * P:(ti + 1) * P], weight(down + c * D),
                                         first=q % inner == 0 and ti == 0, last=q % inner == inner - 1, check=True)
                        if q % inner == inner - 1:
                            last.then_inc(full_sem(name), 1)
                        else:
                            last.then_inc(r_used.sem, 1)

            pe.wait_ge(small_prep, 1)
            pe.wait_ge(pool_prep, 1)
            pe.wait_ge(w_lo, len(pieces))
            with pe.Fori(0, ITERS) as it:
                for s in range(SLOTS):
                    pe.wait_ge(chunk_in[s].sem, chunk_in[s].after(it, "in"))
                    transposed(it, ("T", "c", s), zs[:, s])
                for s in range(SLOTS):
                    transposed(it, ("T", "x0", s), xs[:, s])
                single(it, 0, "x0")

                def input_t(name, src, after):
                    for s in range(SLOTS):
                        pe.wait_ge(normed.sem, normed.after(it, (after, s)))
                        transposed(it, ("T", name, s), src[:, s])

                input_t("x1", xs, "l0")
                mha(it, 0, "x1")
                input_t("x2", xs, "l1")
                single(it, 1, "x2")
                input_t("x3", zs, "x1")
                ffn(it, 0, "x3")
                input_t("x4", xs, "l2")
                mha(it, 1, "x4")
                input_t("x5", xs, "l3")
                mha(it, 2, "x5")
                input_t("x6", xs, "l4")
                ffn(it, 1, "x6")

        @block.scalar
        def _(act):
            go = nc.scalar.activation

            def split_hi(it, name, dst, bias=None, f32=None):
                if f32 is None:
                    act.wait_ge(full_sem(name), full_value(it, name))
                    f32 = bank_of(name)[:]
                if bias is None:
                    go(dst, f32, ACT.Copy).then_inc(hi.sem, 1)
                else:
                    go(dst, f32, ACT.Identity, bias=cb[:, bias:bias + 1]).then_inc(hi.sem, 1)

            def transposed_hi(it, name, dst):
                for s in range(SLOTS):
                    split_hi(it, ("T", name, s), dst[:, s, 0])

            def single(it, a):
                for s in range(SLOTS):
                    split_hi(it, ("v", a, s), qstack[:, s, 0])
                    for x, dst, f32 in (("q", qh, qs), ("k", kh, os_)):
                        if a == 0:
                            act.wait_ge(f32_ready.sem, f32_ready.after(it, (x, 0, s)))
                            split_hi(it, (x, a, s), dst[:, s, 0], f32=f32[:, s])
                        else:
                            split_hi(it, (x, a, s), dst[:, s, 0], bias=C_ONE[a, x])
                for s in range(SLOTS):
                    act.wait_ge(smax.sem, smax.after(it, (a, s)))
                    for i in range(TILES):
                        tile = os_[:, s, i * P:(i + 1) * P]
                        last = go(tile, tile, ACT.Exp, bias=sm[:, s, 1, i:i + 1], scale=ONE_SCALE[a], accum_out=sm[:, s, 2, i:i + 1])
                    last.then_inc(sexp.sem, 1)
                for s in range(SLOTS):
                    act.wait_ge(f32_ready.sem, f32_ready.after(it, ("p", a, s)))
                    split_hi(it, ("p", a, s), kh[:, s, 0], f32=os_[:, s])
                for s in range(SLOTS):
                    name = ("pt", a, s)
                    act.wait_ge(full_sem(name), full_value(it, name))
                    go(qh[:, s].rearrange("p k t -> p (k t)"), bank_of(name)[:].bitcast(F16), ACT.Copy).then_inc(read_sem(name), 1)
                if a:
                    for s in range(SLOTS):
                        split_hi(it, ("o", a, s), oh[:, s, 0])

            def mha(it, m):
                for s in range(SLOTS):
                    if m == 0:
                        act.wait_ge(f32_ready.sem, f32_ready.after(it, ("mk", 0, s)))
                        split_hi(it, ("mk", m, s), kh[:, s, 0], f32=qs[:, s])
                    else:
                        split_hi(it, ("mk", m, s), kh[:, s, 0], bias=C_MHA[m, "k"])
                    if m == 2:
                        act.wait_ge(full_sem(("mq", m, s)), full_value(it, ("mq", m, s)))
                        c = C_MHA[m, "q"]
                        go(qs[:, s], bank_of(("mq", m, s))[:], ACT.Identity, bias=cb[:, c:c + 1])
                    split_hi(it, ("mq", m, s), qh[:, s, 0], bias=C_MHA[m, "q"])

                def place_v(i):
                    name = ("mv", m, i)
                    act.wait_ge(full_sem(name), full_value(it, name))
                    if i >= VRING:
                        act.wait_ge(used_sem(ring_at["t", m, i - VRING, 1]), used_value(it, ring_at["t", m, i - VRING, 1]))
                    for p in range(2):
                        last = go(v_dst(i, 0, p), v_src(name, p), ACT.Copy)
                    last.then_inc(v_hi.sem, 1)

                for i in range(VRING):
                    place_v(i)
                for i in range(n_tiles + 3):
                    if 1 <= i <= n_tiles:
                        q = i - 1
                        name = ("mt", m, q)
                        act.wait_ge(full_sem(name), full_value(it, name))
                        if q >= 2:
                            act.wait_ge(full_sem(("t", m, q - 2, 1)), full_value(it, ("t", m, q - 2, 1)))
                        go(mt[:, q % 2, :], bank_of(name)[:].bitcast(BF16)[:, 0:P], ACT.Copy).then_inc(read_sem(name), 1)
                    if 2 <= i < n_tiles + 2:
                        for b in range(2):
                            name = ("t", m, i - 2, b)
                            ri = ring_at[name]
                            act.wait_ge(full_sem(name), full_value(it, name))
                            if ri >= RING:
                                act.wait_ge(r_lo.sem, r_lo.after(it, rings[ri - RING]))
                                act.wait_ge(used_sem(ri - RING), used_value(it, ri - RING))
                            s, sq = (i - 2) // TILES, 2 * ((i - 2) % TILES) + b
                            bias = {"bias": mk_bias[:, s, sq:sq + 1]} if m == 0 else {}
                            go(r32[:, ri % RING, :], bank_of(name)[:], ACT.Exp, scale=MHA_SCALE, **bias)
                            go(rhl[:, ri % RING, 0, :], bank_of(name)[:], ACT.Exp, scale=MHA_SCALE, **bias).then_inc(read_sem(name), 1)
                    if i >= 3 and i - 3 + VRING < n_tiles:
                        place_v(i - 3 + VRING)
                    if i >= 3 and (i - 3) % 2 == 1:
                        h = (i - 3) // 2
                        name = ("pv", m, h)
                        act.wait_ge(full_sem(name), full_value(it, name))
                        o = bank_of(name)
                        go(rden[0:64, h % 2, :], o[64:128, 0:256], ACT.Ln)
                        go(rden[64:128, h % 2, :], o[0:64, 256:512], ACT.Ln).then_inc(den_ln.sem, 1)
                        act.wait_ge(den_ln.sem, den_ln.after(it, (m, h)))
                        go(rden[:, h % 2, :], rden[:, h % 2, :], ACT.Exp, scale=-1.0).then_inc(den_done.sem, 1)
                if m < 2:
                    for s in range(SLOTS):
                        act.wait_ge(f32_ready.sem, f32_ready.after(it, ("mo", m, s)))
                        split_hi(it, ("mo", m, s), oh[:, s, 0], f32=os_[:, s])
                else:
                    for s in range(SLOTS):
                        act.wait_ge(full_sem(("ot", s)), full_value(it, ("ot", s)))
                        go(flat(ys, s), bank_of(("ot", s))[:], ACT.Copy).then_inc(read_sem(("ot", s)), 1)
                    transposed_hi(it, "o", xt)
                    for s in range(SLOTS):
                        name = ("mw", m, s)
                        act.wait_ge(full_sem(name), full_value(it, name))
                        go(flat(ys, s), bank_of(name)[:], ACT.Gelu).then_inc(read_sem(name), 1)
                    nc.scalar.preload_act_table_set(EXP_LN)

            def ffn(it, f):
                for s in range(SLOTS):
                    act.wait_ge(gate_in.sem, gate_in.after(it, (f, s)))
                    if f == 0:
                        go(gw[:, s, 1], gw[:, s, 0], ACT.Exp).then_inc(gate_exp.sem, 1)
                    else:
                        go(gw[:, s, 2:4], gw[:, s, 0:2], ACT.Exp, scale=-1.0).then_inc(gate_exp.sem, 1)
                if f == 0:
                    for s in range(SLOTS):
                        name = ("gt", s)
                        act.wait_ge(full_sem(name), full_value(it, name))
                        go(gtr[:, s], bank_of(name)[:].bitcast(F16)[:, 0:CHUNK], ACT.Copy).then_inc(read_sem(name), 1)
                n = SLOTS * E * (D0, F1)[f]
                for i in range(n + 1):
                    if i < n:
                        ri = ring_at["h", f, i]
                        name = ("ga" if f else "up", f, i)
                        act.wait_ge(full_sem(name), full_value(it, name))
                        act.wait_ge(r_lo.sem, r_lo.after(it, rings[ri - RING]))
                        if f == 0:
                            c = C_B1 + i % (E * D0)
                            go(r32[:, ri % RING, :], bank_of(name)[:], ACT.Relu, bias=cb[:, c:c + 1]).then_inc(read_sem(name), 1)
                        else:
                            go(r32[:, ri % RING, :], bank_of(name)[:], ACT.Silu).then_inc(read_sem(name), 1)
                    if f == 1 and i >= 1:
                        ri = ring_at["h", f, i - 1]
                        act.wait_ge(read_sem(("up", f, i - 1)), read_value(it, ("up", f, i - 1)))
                        act.wait_ge(used_sem(ri - RING), used_value(it, ri - RING))
                        go(rhl[:, ri % RING, 0, :], r32[:, ri % RING, :], ACT.Copy).then_inc(r_hi.sem, 1)

            for n, (o, c) in enumerate(pieces):
                act.wait_ge(stage_in[n % 2], 16 * (n // 2 + 1))
                if n == 0:
                    act.wait_ge(rot_done, 1)
                go(w[:, 0, o:o + c], stage[n % 2][:, 0:c], ACT.Copy).then_inc(w_hi, 1)
            with act.Fori(0, ITERS) as it:
                nc.scalar.preload_act_table_set(EXP_LN)
                transposed_hi(it, "c", ct)
                transposed_hi(it, "x0", xt)
                single(it, 0)
                transposed_hi(it, "x1", xt)
                mha(it, 0)
                transposed_hi(it, "x2", xt)
                single(it, 1)
                transposed_hi(it, "x3", xt)
                ffn(it, 0)
                transposed_hi(it, "x4", xt)
                mha(it, 1)
                transposed_hi(it, "x5", xt)
                mha(it, 2)
                transposed_hi(it, "x6", xt)
                ffn(it, 1)

        @block.vector
        def _(dve):
            v = nc.vector

            def split_lo(it, name, dst, bias=None, f32=None):
                dve.wait_ge(hi.sem, hi.after(it, name))
                if f32 is not None:
                    v.tensor_tensor(dst[:, 1], f32, dst[:, 0], ALU.subtract).then_inc(lo.sem, 1)
                elif bias is None:
                    v.tensor_tensor(dst[:, 1], bank_of(name)[:], dst[:, 0], ALU.subtract).then_inc(read_sem(name), 1)
                else:
                    v.scalar_tensor_tensor(dst[:, 1], bank_of(name)[:], cb[:, bias:bias + 1], dst[:, 0], ALU.add, ALU.subtract).then_inc(read_sem(name), 1)

            def transposed_lo(it, name, dst):
                for s in range(SLOTS):
                    split_lo(it, ("T", name, s), dst[:, s])

            def norm_stats(it, name, s, src):
                for i in range(TILES):
                    last = v.bn_stats(stats[:, s, i, :], src[:, s, i, :])
                last.then_inc(dve_link, 1)
                dve.wait_ge(dve_link, link_value(it))
                dve.sem_inc(aggr_turn, 1)
                for i in range(TILES):
                    last = v.bn_aggr(mv[:, s, i, :], stats[:, s, i, :])
                last.then_inc(dve_link, 1)
                dve.wait_ge(dve_link, link_value(it))
                v.tensor_scalar(ve[:, s, :], mv[:, s, :, 1], EPS, None, ALU.add).then_inc(variance.sem, 1)

            def norm_apply(it, name, s, src, dst, affine=None):
                dve.wait_ge(rstd_done.sem, rstd_done.after(it, (name, s)))
                for i in range(TILES):
                    last = v.tensor_scalar(dst[:, s, i, :], src[:, s, i, :], mv[:, s, i, 0:1], rstd[:, s, i:i + 1], ALU.subtract, ALU.mult)
                if affine is not None:
                    c = K_LN + affine * D
                    last.then_inc(dve_link, 1)
                    dve.wait_ge(dve_link, link_value(it))
                    v.tensor_tensor(dst[:, s], dst[:, s], repeat(kc[:, c:c + D], TILES), ALU.mult).then_inc(dve_link, 1)
                    dve.wait_ge(dve_link, link_value(it))
                    last = v.tensor_tensor(dst[:, s], dst[:, s], repeat(kc[:, c + D:c + 2 * D], TILES), ALU.add)
                last.then_inc(normed.sem, 1)

            def residual_norm(it, name, step, res):
                for s in range(SLOTS):
                    dve.wait_ge(full_sem((*step, s)), full_value(it, (*step, s)))
                    sem_ = read_sem((*step, s))
                    v.tensor_tensor(flat(ys, s), bank_of((*step, s))[:], flat(res, s), ALU.add).then_inc(sem_, 1)
                    dve.wait_ge(read_sem((*step, s)), read_value(it, (*step, s)))
                    norm_stats(it, name, s, ys)
                for s in range(SLOTS):
                    norm_apply(it, name, s, ys, xs)

            def single(it, a):
                for s in range(SLOTS):
                    if a == 0:
                        for x, dst in (("q", qs), ("k", os_)):
                            dve.wait_ge(full_sem((x, 0, s)), full_value(it, (x, 0, s)))
                            c = C_ONE[0, x]
                            v.scalar_tensor_tensor(tiled(dst[:, s], SEQS), tiled(bank_of((x, 0, s))[:], SEQS), cb[:, c:c + 1],
                                                   repeat(kc[:, K_ROPE:K_ROPE + SEQ], SEQS), ALU.add, ALU.mult).then_inc(read_sem((x, 0, s)), 1)
                            dve.wait_ge(read_sem((x, 0, s)), read_value(it, (x, 0, s)))
                            dve.sem_inc(f32_ready.sem, 1)
                    split_lo(it, ("v", a, s), qstack[:, s])
                    for x, dst, f32 in (("q", qh, qs), ("k", kh, os_)):
                        if a == 0:
                            split_lo(it, (x, a, s), dst[:, s], f32=f32[:, s])
                        else:
                            split_lo(it, (x, a, s), dst[:, s], bias=C_ONE[a, x])
                for s in range(SLOTS):
                    name = ("s", a, s)
                    dve.wait_ge(full_sem(name), full_value(it, name))
                    if a == 0:
                        dve.wait_ge(split_sem(("k", a, s)), split_value(it, ("k", a, s)))
                    v.tensor_tensor(tiled(os_[:, s]), tiled(bank_of(name)[:]), repeat(kc[:, K_CROSS:K_CROSS + P], TILES), ALU.add).then_inc(read_sem(name), 1)
                    dve.wait_ge(read_sem(name), read_value(it, name))
                    v.reduce_max(sm[:, s, 0, :], tiled(os_[:, s]), AX).then_inc(dve_link, 1)
                    dve.wait_ge(dve_link, link_value(it))
                    v.tensor_scalar(sm[:, s, 1, :], sm[:, s, 0, :], -ONE_SCALE[a], None, ALU.mult).then_inc(smax.sem, 1)
                for s in range(SLOTS):
                    dve.wait_ge(sexp.sem, sexp.after(it, (a, s)))
                    v.reciprocal(sm[:, s, 3, :], sm[:, s, 2, :]).then_inc(dve_link, 1)
                    dve.wait_ge(dve_link, link_value(it))
                    v.tensor_tensor(tiled(os_[:, s]), tiled(os_[:, s]), spread(sm[:, s, 3, :], P), ALU.mult).then_inc(f32_ready.sem, 1)
                for s in range(SLOTS):
                    split_lo(it, ("p", a, s), kh[:, s], f32=os_[:, s])
                if a == 0:
                    residual_norm(it, "l0", ("o", 0), xs)
                else:
                    for s in range(SLOTS):
                        split_lo(it, ("o", a, s), oh[:, s])
                    for s in range(SLOTS):
                        name = ("wo", a, s)
                        dve.wait_ge(full_sem(name), full_value(it, name))
                        v.tensor_tensor(flat(zs, s), bank_of(name)[:], flat(xs, s), ALU.add).then_inc(read_sem(name), 1)
                        dve.wait_ge(read_sem(name), read_value(it, name))
                        dve.sem_inc(normed.sem, 1)

            def masks(it):
                for s in range(SLOTS):
                    dve.wait_ge(chunk_in[s].sem, chunk_in[s].after(it, "in"))
                    v.tensor_copy(os_[:, s], kmask8[:, s]).then_inc(dve_link, 1)
                    dve.wait_ge(dve_link, link_value(it))
                    v.reduce_max(seq_any[:, s], tiled(os_[:, s], SEQS), AX).then_inc(dve_link, 1)
                    dve.wait_ge(dve_link, link_value(it))
                    v.tensor_tensor(tiled(os_[:, s], SEQS), tiled(os_[:, s], SEQS), spread(seq_any[:, s], SEQ), ALU.subtract).then_inc(dve_link, 1)
                    dve.wait_ge(dve_link, link_value(it))
                    v.tensor_scalar(amask[:, s], os_[:, s], -MASKED / MHA_SCALE, None, ALU.mult)
                    v.tensor_tensor(mk_bias[:, s], mk8[:, s], seq_any[:, s], ALU.subtract).then_inc(dve_link, 1)
                    dve.wait_ge(dve_link, link_value(it))
                    v.tensor_scalar(mk_bias[:, s], mk_bias[:, s], -MASKED, None, ALU.mult).then_inc(masks_ready.sem, 1)

            def mha(it, m):
                for s in range(SLOTS):
                    if m == 0:
                        name = ("mk", 0, s)
                        dve.wait_ge(full_sem(name), full_value(it, name))
                        c = C_MHA[0, "k"]
                        v.scalar_tensor_tensor(qs[:, s], bank_of(name)[:], cb[:, c:c + 1], kmask8[:, s], ALU.add, ALU.mult).then_inc(read_sem(name), 1)
                        dve.wait_ge(read_sem(name), read_value(it, name))
                        dve.sem_inc(f32_ready.sem, 1)
                        split_lo(it, name, kh[:, s], f32=qs[:, s])
                    else:
                        split_lo(it, ("mk", m, s), kh[:, s], bias=C_MHA[m, "k"])
                    split_lo(it, ("mq", m, s), qh[:, s], bias=C_MHA[m, "q"])

                def place_v(i):
                    name = ("mv", m, i)
                    dve.wait_ge(v_hi.sem, v_hi.after(it, (m, i)))
                    for p in range(2):
                        last = v.tensor_tensor(v_dst(i, 1, p), v_src(name, p), v_dst(i, 0, p), ALU.subtract)
                    last.then_inc(read_sem(name), 1)

                def maxima(i):
                    s, ti = i // TILES, i % TILES
                    for hb in range(2):
                        name = ("n", m, i, hb)
                        dve.wait_ge(full_sem(name), full_value(it, name))
                        v.reduce_max(mx[:, s, ti, 8 * hb:8 * hb + 8], tiled(bank_of(name)[:], 8), AX).then_inc(read_sem(name), 1)
                    dve.wait_ge(read_sem(("n", m, i, 1)), read_value(it, ("n", m, i, 1)))
                    if i >= 2:
                        dve.wait_ge(full_sem(("mt", m, i - 2)), full_value(it, ("mt", m, i - 2)))
                    v.tensor_copy(mhl[:, i % 2, 0:HEADS], mx[:, s, ti, :]).then_inc(dve_link, 1)
                    dve.wait_ge(dve_link, link_value(it))
                    v.tensor_tensor(mhl[:, i % 2, HEADS:2 * HEADS], mx[:, s, ti, :], mhl[:, i % 2, 0:HEADS], ALU.subtract).then_inc(max_split.sem, 1)

                for i in range(VRING):
                    place_v(i)
                for i in range(n_tiles + 3):
                    if i < n_tiles:
                        maxima(i)
                    if i >= 3 and i - 3 + VRING < n_tiles:
                        place_v(i - 3 + VRING)
                    if i >= 3 and (i - 3) % 2 == 1:
                        h = (i - 3) // 2
                        name = ("pv", m, h)
                        dve.wait_ge(den_done.sem, den_done.after(it, (m, h)))
                        o, s, c = bank_of(name), h // 2, (h % 2) * 256
                        v.tensor_tensor(os_[0:64, s, c:c + 256], o[0:64, 0:256], rden[0:64, h % 2, :], ALU.mult)
                        v.tensor_tensor(os_[64:128, s, c:c + 256], o[64:128, 256:512], rden[64:128, h % 2, :], ALU.mult).then_inc(read_sem(name), 1)
                        if h % 2 == 1:
                            dve.wait_ge(read_sem(name), read_value(it, name))
                            if m == 2:
                                v.tensor_tensor(os_[:, s], os_[:, s], qs[:, s], ALU.add).then_inc(f32_ready.sem, 1)
                            else:
                                dve.sem_inc(f32_ready.sem, 1)
                if m < 2:
                    for s in range(SLOTS):
                        split_lo(it, ("mo", m, s), oh[:, s], f32=os_[:, s])
                    residual_norm(it, ("l1", "l3")[m], ("mw", m), xs)
                    return
                for s in range(SLOTS):
                    dve.wait_ge(read_sem(("ot", s)), read_value(it, ("ot", s)))
                    norm_stats(it, "la", s, ys)
                for s in range(SLOTS):
                    norm_apply(it, "la", s, ys, zs, 0)
                transposed_lo(it, "o", xt)
                for s in range(SLOTS):
                    dve.wait_ge(read_sem(("mw", m, s)), read_value(it, ("mw", m, s)))
                    v.tensor_tensor(flat(ys, s), flat(ys, s), flat(zs, s), ALU.add).then_inc(dve_link, 1)
                    dve.wait_ge(dve_link, link_value(it))
                    norm_stats(it, "lb", s, ys)
                for s in range(SLOTS):
                    norm_apply(it, "lb", s, ys, zs, 2)
                    dve.wait_ge(normed.sem, normed.after(it, ("lb", s)))
                    v.tensor_tensor(flat(ys, s), flat(zs, s), flat(xs, s), ALU.add).then_inc(dve_link, 1)
                    dve.wait_ge(dve_link, link_value(it))
                    norm_stats(it, "l4", s, ys)
                for s in range(SLOTS):
                    norm_apply(it, "l4", s, ys, xs)

            def gates_dense(it, s):
                name = ("g", 0, s)
                dve.wait_ge(full_sem(name), full_value(it, name))
                lg = bank_of(name)[:, 0:TILES * E].rearrange("p (t e) -> p t e", e=E)
                v.reduce_max(gm[:, s, 0], lg, AX).then_inc(dve_link, 1)
                dve.wait_ge(dve_link, link_value(it))
                v.tensor_tensor(gw[:, s, 0], lg, spread(gm[:, s, 0], E), ALU.subtract).then_inc(read_sem(name), 1)
                dve.wait_ge(read_sem(name), read_value(it, name))
                dve.sem_inc(gate_in.sem, 1)
                dve.wait_ge(gate_exp.sem, gate_exp.after(it, (0, s)))
                v.reduce_sum(gm[:, s, 1], gw[:, s, 1], AX).then_inc(dve_link, 1)
                dve.wait_ge(dve_link, link_value(it))
                v.reciprocal(gm[:, s, 2], gm[:, s, 1]).then_inc(dve_link, 1)
                dve.wait_ge(dve_link, link_value(it))
                v.tensor_tensor(gates[:, s], gw[:, s, 1], spread(gm[:, s, 2], E), ALU.mult).then_inc(dve_link, 1)
                dve.wait_ge(dve_link, link_value(it))
                v.memset(gstack[:, s], 0.0).then_inc(dve_link, 1)
                dve.wait_ge(dve_link, link_value(it))
                v.tensor_copy(gstack[:, s, :, 64:64 + E], gates[:, s])
                v.tensor_copy(gstack[:, s, :, 0:E], gates[:, s]).then_inc(dve_link, 1)
                dve.wait_ge(dve_link, link_value(it))
                v.tensor_tensor(gstack[:, s, :, 32:32 + E], gates[:, s], gstack[:, s, :, 0:E], ALU.subtract).then_inc(gate_stack.sem, 1)

            def gates_top2(it, s):
                name = ("g", 1, s)
                dve.wait_ge(full_sem(name), full_value(it, name))
                t1, t2, e1, e2, lg, ab, one1, masked, k1, k2, tmp, one2 = (gw[:, s, n] for n in range(12))
                m1, m2, c1, c2, s1, s2, r1, r2 = (gm[:, s, n] for n in range(8))
                iota = repeat(kc[:, K_IOTA:K_IOTA + E], TILES)
                tt, stt = v.tensor_tensor, v.scalar_tensor_tensor

                def first_of(vals, top, c, onehot):
                    tt(onehot, vals, spread(top, E), ALU.is_equal).then_inc(dve_link, 1)
                    dve.wait_ge(dve_link, link_value(it))
                    stt(tmp, onehot, -float(E), iota, ALU.mult, ALU.add).then_inc(dve_link, 1)
                    dve.wait_ge(dve_link, link_value(it))
                    v.tensor_reduce(c, tmp, AX, ALU.min).then_inc(dve_link, 1)
                    dve.wait_ge(dve_link, link_value(it))
                    tt(onehot, tmp, spread(c, E), ALU.is_equal).then_inc(dve_link, 1)
                    dve.wait_ge(dve_link, link_value(it))

                def within(top, t_, keep):
                    tt(tmp, ab, spread(top, E), ALU.max).then_inc(dve_link, 1)
                    dve.wait_ge(dve_link, link_value(it))
                    stt(keep, tmp, 0.02, t_, ALU.mult, ALU.is_ge).then_inc(dve_link, 1)
                    dve.wait_ge(dve_link, link_value(it))

                v.tensor_copy(lg, bank_of(name)[:, 0:TILES * E].rearrange("p (t e) -> p t e", e=E)).then_inc(read_sem(name), 1)
                dve.wait_ge(read_sem(name), read_value(it, name))
                v.reduce_max(m1, lg, AX).then_inc(dve_link, 1)
                dve.wait_ge(dve_link, link_value(it))
                stt(ab, lg, -1.0, lg, ALU.mult, ALU.max).then_inc(dve_link, 1)
                dve.wait_ge(dve_link, link_value(it))
                first_of(lg, m1, c1, one1)
                tt(t1, spread(m1, E), lg, ALU.subtract).then_inc(dve_link, 1)
                dve.wait_ge(dve_link, link_value(it))
                within(m1, t1, k1)
                stt(masked, one1, -1e30, lg, ALU.mult, ALU.add).then_inc(dve_link, 1)
                dve.wait_ge(dve_link, link_value(it))
                v.reduce_max(m2, masked, AX).then_inc(dve_link, 1)
                dve.wait_ge(dve_link, link_value(it))
                first_of(masked, m2, c2, one2)
                tt(t2, spread(m2, E), masked, ALU.subtract).then_inc(dve_link, 1)
                dve.wait_ge(dve_link, link_value(it))
                within(m2, t2, k2)
                dve.sem_inc(gate_in.sem, 1)
                dve.wait_ge(gate_exp.sem, gate_exp.after(it, (1, s)))
                tt(k1, k1, e1, ALU.mult).then_inc(dve_link, 1)
                dve.wait_ge(dve_link, link_value(it))
                tt(k2, k2, e2, ALU.mult).then_inc(dve_link, 1)
                dve.wait_ge(dve_link, link_value(it))
                v.reduce_sum(s1, k1, AX).then_inc(dve_link, 1)
                dve.wait_ge(dve_link, link_value(it))
                v.reduce_sum(s2, k2, AX).then_inc(dve_link, 1)
                dve.wait_ge(dve_link, link_value(it))
                v.reciprocal(r1, s1).then_inc(dve_link, 1)
                dve.wait_ge(dve_link, link_value(it))
                v.reciprocal(r2, s2).then_inc(dve_link, 1)
                dve.wait_ge(dve_link, link_value(it))
                tt(one1, one1, spread(r1, E), ALU.mult).then_inc(dve_link, 1)
                dve.wait_ge(dve_link, link_value(it))
                tt(one2, one2, spread(r2, E), ALU.mult).then_inc(dve_link, 1)
                dve.wait_ge(dve_link, link_value(it))
                tt(gates[:, s], one1, one2, ALU.add).then_inc(dve_link, 1)
                dve.wait_ge(dve_link, link_value(it))

            def ffn(it, f):
                for s in range(SLOTS):
                    (gates_dense, gates_top2)[f](it, s)
                if f == 0:
                    for s in range(SLOTS):
                        name = ("gb", s)
                        dve.wait_ge(full_sem(name), full_value(it, name))
                        v.tensor_tensor(flat(ys, s), bank_of(name)[:], flat(zs, s), ALU.add).then_inc(read_sem(name), 1)
                        dve.wait_ge(read_sem(name), read_value(it, name))
                        v.tensor_tensor(flat(ys, s), flat(ys, s), flat(xs, s), ALU.add).then_inc(dve_link, 1)
                        dve.wait_ge(dve_link, link_value(it))
                inner = (D0, F1)[f]
                n = SLOTS * E * inner
                for i in range(n + FLAG):
                    if i < n:
                        ri = ring_at["h", f, i]
                        f32, slot = r32[:, ri % RING, :], ri % RING
                        if f == 0:
                            dve.wait_ge(read_sem(("up", f, i)), read_value(it, ("up", f, i)))
                            dve.wait_ge(used_sem(ri - RING), used_value(it, ri - RING))
                            v.tensor_copy(rhl[:, slot, 0, :], f32).then_inc(r_hi.sem, 1)
                        else:
                            dve.wait_ge(read_sem(("ga", f, i)), read_value(it, ("ga", f, i)))
                            dve.wait_ge(full_sem(("up", f, i)), full_value(it, ("up", f, i)))
                            v.tensor_tensor(f32, bank_of(("up", f, i))[:], f32, ALU.mult).then_inc(read_sem(("up", f, i)), 1)
                    if i >= FLAG and (i - FLAG) % inner == inner - 1:
                        e = (i - FLAG) // inner
                        s, e = e // E, e % E
                        name = ("y", f, (i - FLAG) // inner)
                        dve.wait_ge(full_sem(name), full_value(it, name))
                        src = xs if f and e == 0 else ys
                        for ti in range(TILES):
                            last = v.scalar_tensor_tensor(ys[:, s, ti, :], bank_of(name)[:, ti * P:(ti + 1) * P], gates[:, s, ti, e:e + 1],
                                                          src[:, s, ti, :], ALU.mult, ALU.add)
                        last.then_inc(read_sem(name), 1)
                        dve.wait_ge(read_sem(name), read_value(it, name))
                        if e == E - 1:
                            norm_stats(it, ("l2", "l5")[f], s, ys)
                for s in range(SLOTS):
                    norm_apply(it, ("l2", "l5")[f], s, ys, xs)

            for sig in read + acc_read:
                dve.sem_inc(sig.sem, 1)
            zf = zs[:].rearrange("p s t d -> p (s t d)")
            yf = ys[:].rearrange("p s t d -> p (s t d)")
            first_links = prep_link
            prep_count = [0]

            def after(ins):
                prep_count[0] += 1
                ins.then_inc(first_links, 1)
                dve.wait_ge(first_links, prep_count[0])

            dve.wait_ge(consts_in, 80)
            c16 = r32[:].rearrange("p r c -> p (r c)")
            v.tensor_copy(ident16[:], kc[:, K_ID:K_ID + P])
            v.tensor_copy(identb[:], kc[:, K_ID:K_ID + P])
            v.tensor_copy(negsel[:].rearrange("p j c -> p (j c)"), c16[:, S_SEL:S_SEL + PAIRS * P])
            v.tensor_copy(ones_rows[:], c16[:, S_ONES:S_ONES + P])
            v.memset(half[:], -0.5)
            v.tensor_copy(rb[:, 0:1024], yf[:, 0:1024])
            v.tensor_copy(rb[:, 1024:R_B2], zf[:, 0:R_B2 - 1024])
            after(v.tensor_copy(b2[:], zf[:, R_B2 - 1024:NR - 1024]))
            v.tensor_tensor(rb[32:64, 0:1024], yf[32:64, 0:1024], rb[32:64, 0:1024], ALU.subtract)
            v.tensor_tensor(rb[32:64, 1024:R_B2], zf[32:64, 0:R_B2 - 1024], rb[32:64, 1024:R_B2], ALU.subtract)
            after(v.tensor_tensor(b2[64:96], zf[64:96, R_B2 - 1024:NR - 1024], b2[64:96], ALU.subtract))
            for n in range(2):
                last = v.scalar_tensor_tensor(cb[:, n:n + 1], cb[:, C_PART + n:C_PART + n + 1], kc[:, K_SIGN:K_SIGN + 1], cb[:, n:n + 1], ALU.mult, ALU.add)
            after(last)
            dve.wait_ge(stage_in[0], 16)
            pair_of = lambda ap: ap.rearrange("p (c two) -> p two c", two=2)
            wq, tmp = pair_of(stage[0][:, 0:2 * D]), pair_of(yf[:, 0:2 * D])
            v.tensor_tensor(tmp[:, 0], wq[:, 0], wq[:, 1], ALU.subtract)
            after(v.tensor_tensor(tmp[:, 1], wq[:, 1], wq[:, 0], ALU.add))
            v.tensor_copy(stage[0][:, 0:2 * D], yf[:, 0:2 * D]).then_inc(rot_done, 1)
            dve.wait_ge(rot_done, 1)
            dve.sem_inc(small_prep, 1)
            for n, (o, c) in enumerate(pieces):
                dve.wait_ge(w_hi, n + 1)
                v.tensor_tensor(w[:, 1, o:o + c], stage[n % 2][:, 0:c], w[:, 0, o:o + c], ALU.subtract).then_inc(w_lo, 1)
            with dve.Fori(0, ITERS) as it:
                links[0] = 0
                masks(it)
                transposed_lo(it, "c", ct)
                transposed_lo(it, "x0", xt)
                single(it, 0)
                transposed_lo(it, "x1", xt)
                mha(it, 0)
                transposed_lo(it, "x2", xt)
                single(it, 1)
                transposed_lo(it, "x3", xt)
                ffn(it, 0)
                transposed_lo(it, "x4", xt)
                mha(it, 1)
                transposed_lo(it, "x5", xt)
                mha(it, 2)
                transposed_lo(it, "x6", xt)
                ffn(it, 1)
            assert links[0] == LINKS, links[0]

        @block.gpsimd
        def _(pool):
            g = nc.gpsimd

            def norms(it, name):
                for s in range(SLOTS):
                    pool.wait_ge(variance.sem, variance.after(it, (name, s)))
                    g.tensor_tensor(rstd[:, s, :], ve[:, s, :], half[:], ALU.pow).then_inc(rstd_done.sem, 1)

            def part_lo(it, r):
                ri = ring_at[r] % RING
                if r[0] == "t":
                    pool.wait_ge(read_sem(r), read_value(it, r))
                else:
                    pool.wait_ge(r_hi.sem, r_hi.after(it, r))
                g.tensor_tensor(rhl[:, ri, 1, :], r32[:, ri, :], rhl[:, ri, 0, :], ALU.subtract).then_inc(r_lo.sem, 1)

            def mha(it, m):
                for i in range(n_tiles):
                    for b in range(2):
                        part_lo(it, ("t", m, i, b))

            def ffn(it, f):
                for i in range(SLOTS * E * (D0, F1)[f]):
                    part_lo(it, ("h", f, i))

            last = g.memset(vm[:].rearrange("p a k s c -> p (a k s c)"), 0.0)
            last = g.memset(mhl[:].rearrange("p a c -> p (a c)"), 0.0)
            last.then_inc(pool_cleared, 1)
            pool.wait_ge(pool_cleared, 1)
            for p in range(2):
                for h in range(VRING):
                    for sq in range(2):
                        for vp in range(2):
                            c = 64 + 32 * p + vp * (4 * VSTEP - VBACK - 64)
                            row = vm[64 * p:64 * p + 64, h, 0, sq, c:c + 4 * (VSTEP + 1)].rearrange("q (g w) -> q g w", g=4)
                            last = g.memset(row[:, :, 0:4 * HD:4], 1.0)
                last.then_inc(pool_cleared, 1)
                pool.wait_ge(pool_cleared, 2 + p)
            pool.wait_ge(w_lo, len(pieces))
            g.memset(kstack[:].rearrange("p s v g u t -> p (s v g u t)"), 0.0).then_inc(pool_prep, 1)
            with pool.Fori(0, ITERS) as it:
                norms(it, "l0")
                mha(it, 0)
                norms(it, "l1")
                ffn(it, 0)
                norms(it, "l2")
                mha(it, 1)
                norms(it, "l3")
                mha(it, 2)
                norms(it, "la")
                norms(it, "lb")
                norms(it, "l4")
                ffn(it, 1)
                norms(it, "l5")


EXP_LN = "natural_log_exp_and_others"


def _arrays(inp):
    import numpy as np

    f = {k: np.asarray(a) for k, a in inp.items()}
    rows = np.empty(D, np.int64)
    vcols = np.empty(D, np.int64)
    for h in range(HEADS):
        for i in range(HD):
            rows[row_of(h, i)] = h * HD + i
            vcols[vcol_of(h, i)] = h * HD + i
    qkv = f["L1_attn_w_qkv"]
    bqkv = f["L1_attn_b_qkv"]
    proj = [f["L0_attn_Wq"].T, f["L0_attn_Wk"].T, f["L0_attn_Wv"].T,
            f["L0_ffn_Wq"], f["L0_ffn_Wk"], f["L0_ffn_Wv"], f["L0_ffn_Wo"],
            f["L0_xattn_Wq"].T[:, rows], f["L0_xattn_Wk"].T[:, rows], f["L0_xattn_Wv"].T[:, vcols], f["L0_xattn_Wo"].T[rows],
            qkv[:, 0:D][:, rows], qkv[:, D:2 * D][:, rows], qkv[:, 2 * D:][:, vcols], f["L1_attn_w_out"][rows],
            f["L1_xattn_Wq"][:, rows], f["L1_xattn_Wk"][:, rows], f["L1_xattn_Wv"][rows][:, vcols], f["L1_xattn_Wo"]]
    weights = np.concatenate(proj + [
        f["L0_ffn_Wg"], f["L1_ffn_router_w"].T,
        f["L0_ffn_W1"].transpose(1, 0, 2).reshape(D, -1),
        f["L0_ffn_W2"].reshape(E, D0, P, D).transpose(2, 0, 1, 3).reshape(P, -1),
        f["L1_ffn_w_gate"].transpose(2, 0, 1).reshape(D, -1),
        f["L1_ffn_w_up"].transpose(2, 0, 1).reshape(D, -1),
        f["L1_ffn_w_down"].transpose(2, 0, 1).reshape(F1, P, E, D).transpose(1, 2, 0, 3).reshape(P, -1)], axis=1)
    assert weights.shape == (P, NW)
    row_bias = np.zeros((P, NR), np.float32)
    vecs = [f["L0_attn_bv"], f["L0_ffn_bv"], f["L0_ffn_bo"],
            f["L0_xattn_bv"][vcols], f["L0_xattn_bo"], bqkv[2 * D:][vcols], f["L1_attn_b_out"],
            f["L1_xattn_bv"][vcols], f["L1_xattn_bo"], f["L0_ffn_bg"]]
    for r in (0, 32):
        row_bias[r, 0:R_B2] = np.concatenate(vecs)
    for r in (0, 32, 64):
        row_bias[r:r + E, R_B2:] = f["L0_ffn_b2"]
    partner = np.arange(D) ^ 1
    col = [f["L0_attn_bq"], f["L0_attn_bk"], f["L0_ffn_bq"], f["L0_ffn_bk"],
           f["L0_xattn_bq"][rows], f["L0_xattn_bk"][rows], bqkv[0:D][rows], bqkv[D:2 * D][rows],
           f["L1_xattn_bq"][rows], f["L1_xattn_bk"][rows]]
    col_bias = np.concatenate([np.stack(col, 1), f["L0_ffn_b1"].reshape(E * D0, P).T,
                               np.stack([f["L0_attn_bq"][partner], f["L0_attn_bk"][partner]], 1)], axis=1)
    k, k16 = np.zeros((P, NK), np.float32), np.zeros((P, NS), np.float32)
    k[:, K_ID:K_ID + P] = np.eye(P)
    k[np.arange(P), K_PERM + rows] = 1
    seq = np.arange(P) // SEQ
    k[:, K_CROSS:K_CROSS + P] = np.where(seq[:, None] == seq[None, :], 0.0, -1e30)
    half_dim = D // 2
    inv = np.float32(10000.0) ** (np.arange(0, half_dim, 2, dtype=np.float32) / np.float32(half_dim))
    rad = np.arange(SEQ, dtype=np.float32)[:, None] / inv
    table = np.repeat(np.stack((np.sin(rad), np.cos(rad)), axis=-1).reshape(SEQ, -1), 2, axis=-1)
    k[:, K_ROPE:K_ROPE + SEQ] = table.T
    for j in range(PAIRS):
        for p in range(2):
            r = 4 * (j % 4) + 2 * (j // 4) + p
            c = S_SEL + j * P + 64 * p
            k16[[r, HEADS + r], c:c + 64] = -1
    k16[[0, 32], S_ONES:S_ONES + P] = 1
    k[:, K_SIGN] = np.where(np.arange(P) % 2 == 0, -1, 1)
    k[:, K_IOTA:K_IOTA + E] = np.arange(E)
    for n, name in enumerate(("g0", "b0", "g1", "b1")):
        k[:, K_LN + n * D:K_LN + (n + 1) * D] = f["L1_xattn_" + name][None, :]
    mask = f["mask_BxS2_bf1"].view(np.uint8)
    return {
        "x": f["x"].reshape(TOKENS, D), "ctx": f["ctx_1024"].reshape(TOKENS, D),
        "mask_row": mask.reshape(1, TOKENS), "mask_cols": np.concatenate([mask.T, mask.T], axis=0),
        "weights": weights, "row_bias": row_bias, "col_bias": col_bias, "consts": k, "consts16": k16,
    }


def kernel(**inputs):
    import numpy as _np
    import concourse.bacc as _bacc
    from concourse.bass_utils import run_bass_kernel_spmd as _run

    nc = _bacc.Bacc("TRN2", target_bir_lowering=False, num_devices=1)
    arrays, t = {}, {}
    for name, a in _arrays(inputs).items():
        a = _np.ascontiguousarray(a)
        arrays["in_" + name] = a
        t[name] = nc.dram_tensor("in_" + name, a.shape, mybir.dt.from_np(a.dtype), kind="ExternalInput").ap()
    t["out"] = nc.dram_tensor("out", (TOKENS, D), F32, kind="ExternalOutput").ap()
    build(nc, t)
    r = _run(nc, [arrays], core_ids=[0])
    return r.results[0]["out"].reshape(BATCH, SEQ, D)
```

```python
from contextlib import ExitStack

import concourse.bass as bass
from concourse import mybir

F32 = mybir.dt.float32
F16 = mybir.dt.float16
BF16 = mybir.dt.bfloat16
U8 = mybir.dt.uint8
ALU = mybir.AluOpType
ACT = mybir.ActivationFunctionType
AX = mybir.AxisListType.X

P = 128
D = 128
SEQ = 64
BATCH = 32
TOKENS = BATCH * SEQ
CHUNK = 512
TILES = CHUNK // P
SEQS = CHUNK // SEQ
SLOTS = 2
ITERS = TOKENS // (CHUNK * SLOTS)
HEADS = 16
HD = D // HEADS
PAIRS = HEADS // 2
GROUPS = 4
E = 8
D0 = 512 // P
F1 = 256 // P
BANKS = 5
Y_BANKS, PV_BANKS = 2, 1
VRING = 2
H_RING, T_RING = 4, 3
VSTEP = 188
VBACK = 60
VW = 32 + PAIRS * (VSTEP + 1)
EPS = 1e-5
MHA_SCALE = float(HD) ** -0.5
ONE_SCALE = (0.125, float(D) ** -0.5)
MASKED = -1e8
LINKS = 152

W_ONE = {(0, "q"): 0, (0, "k"): 1, (0, "v"): 2, (1, "q"): 3, (1, "k"): 4, (1, "v"): 5, (1, "o"): 6}
W_MHA = {(m, w): 7 + 4 * m + n for m in range(3) for n, w in enumerate("qkvo")}
NPROJ = 19
W_G0 = NPROJ * D
W_G1 = W_G0 + E
W_UP0 = W_G1 + E
W_DN0 = W_UP0 + E * D0 * D
W_GA1 = W_DN0 + E * D0 * D
W_UP1 = W_GA1 + E * F1 * D
W_DN1 = W_UP1 + E * F1 * D
NW = W_DN1 + E * F1 * D
R_ONE = {(0, "v"): 0, (1, "v"): 1, (1, "o"): 2}
R_MHA = {(m, w): 3 + 2 * m + n for m in range(3) for n, w in enumerate("vo")}
R_G0 = 9 * D
R_B2 = R_G0 + E
NR = R_B2 + D
C_ONE = {(0, "q"): 0, (0, "k"): 1, (1, "q"): 2, (1, "k"): 3}
C_MHA = {(m, w): 4 + 2 * m + n for m in range(3) for n, w in enumerate("qk")}
C_B1 = 10
C_PART = C_B1 + E * D0
NC = C_PART + 2
K_ID, K_PERM, K_CROSS, K_ROPE, K_SIGN = 0, 128, 256, 384, 448
K_IOTA = K_SIGN + 1
K_LN = K_IOTA + E
NK = K_LN + 4 * D
S_SEL, S_ONES, NS = 0, PAIRS * D, PAIRS * D + D


def row_of(h, i):
    p, j = h % 2, h // 2
    return 64 * (j // 4) + 32 * p + 4 * i + j % 4


def vcol_of(h, i):
    return 64 * (h % 2) + 8 * (h // 2) + i


STEP = ("step", None)


def tr_steps(name, s):
    yield ("bank", ("T", name, s))
    yield ("split", ("T", name, s))
    yield STEP


def single_steps(a, s):
    for w in "qkv":
        yield ("bank", (w, a, s))
    for w in "vqk":
        yield ("split", (w, a, s))
    yield STEP
    yield ("bank", ("s", a, s))
    yield STEP
    yield ("split", ("p", a, s))
    yield STEP
    yield STEP
    yield ("bank", ("pt", a, s))
    yield STEP
    yield ("bank", ("o", a, s))
    if a:
        yield ("split", ("o", a, s))
        yield STEP
        yield ("bank", ("wo", a, s))
        yield STEP
    else:
        yield STEP


def prepare_steps(m, s):
    if m == 1:
        yield ("bank", ("mk", m, s))
        yield ("split", ("mk", m, s))
    yield ("bank", ("mq", m, s))
    yield ("split", ("mq", m, s))
    yield STEP


def leave_steps(m, s):
    if m < 2:
        yield ("split", ("mo", m, s))
        yield STEP
        yield ("bank", ("mw", m, s))
        yield STEP
        yield STEP
    else:
        yield ("bank", ("ot", s))
        yield STEP
        yield STEP
        yield from tr_steps("o", s)
        yield ("bank", ("mw", m, s))
        yield STEP
        yield STEP
        yield STEP
        yield STEP
        yield STEP


def gates_steps(f, s):
    yield ("bank", ("g", f, s))
    if f == 0:
        yield STEP
        yield STEP
        yield ("bank", ("gt", s))
        yield STEP
        yield ("bank", ("gb", s))
        yield STEP
    else:
        yield STEP
        yield STEP
        yield STEP


def enter_steps(s):
    yield from tr_steps("c", s)
    for m in (0, 2):
        yield ("bank", ("mk", m, s))
        yield ("split", ("mk", m, s))
    yield STEP
    yield from tr_steps("x0", s)
    yield from single_steps(0, s)
    yield STEP
    yield from tr_steps("x1", s)
    yield from prepare_steps(0, s)


def between_steps(k, s):
    if k == 0:
        yield from leave_steps(0, s)
        yield from tr_steps("x2", s)
        yield from single_steps(1, s)
        yield from tr_steps("x3", s)
        yield from gates_steps(0, s)
    elif k == 1:
        yield STEP
        yield STEP
        yield from tr_steps("x4", s)
        yield from prepare_steps(1, s)
    elif k == 2:
        yield from leave_steps(1, s)
        yield from tr_steps("x5", s)
        yield from prepare_steps(2, s)
    elif k == 3:
        yield from leave_steps(2, s)
        yield from tr_steps("x6", s)
        yield from gates_steps(1, s)
    else:
        yield STEP
        yield STEP


def mha_steps(m, s):
    for n in range(TILES + 3):
        i = s * TILES + n
        if n < TILES:
            yield ("bank", ("n", m, i, 0))
            yield ("bank", ("n", m, i, 1))
        yield STEP
        if n < VRING:
            yield ("bank", ("mv", m, i))
        if 1 <= n <= TILES:
            yield ("bank", ("mt", m, i - 1))
        yield STEP
        for b in range(2):
            if 2 <= n < TILES + 2:
                yield ("bank", ("t", m, i - 2, b))
                yield ("ring", ("t", m, i - 2, b))
            yield STEP
        if n >= 3 and (n - 3) % 2 == 0:
            yield ("pv", ("pv", m, (i - 3) // 2))
        if n >= 3 and n - 3 + VRING < TILES:
            yield ("bank", ("mv", m, i - 3 + VRING))
        yield STEP


def ffn_steps(f, s):
    inner = (D0, F1)[f]
    total = E * inner
    for n in range(total + FLAG):
        i = s * total + n
        if n < total:
            yield ("bank", ("up", f, i))
            if f == 1:
                yield ("bank", ("ga", f, i))
            yield ("ring", ("h", f, i))
        if n >= FLAG and (n - FLAG) % inner == 0:
            yield ("acc", ("y", f, (i - FLAG) // inner))
        yield STEP


ORDER = """
    e0*2 e1 e0 e1 e0 e1 e0*3 e1 e0*3 e1 e0*2 e1*4 a00*17 e1 a00*5 e1 a00*12 e1 a00 b00*2 a01 b00 a01*6 b00 a01*6
    b00 a01*5 b00 a01 b00*2 a01*4 b00 a01*2 b00 a01*5 b00 a01*4 b00 a01 b00*2 f00 b01 f00*2 b00 b01 f00 b00 b01
    f00*2 b01 f00*2 b01 f00*3 b01 f00 b01*2 f00*3 b01 f00*2 b01 f00*2 b01 f00*2 b01 f00*2 b01*2 f00*2 b01 f00 b01
    f00*9 b10*2 f01*10 b10 f01*3 b10 f01*12 a10 f01*4 a10 f01*4 a10*5 f01*2 b11 a10*4 b11 a10*7 b11 a10*2 b11
    a10*15 b20 a11*6 b20 a11*6 b20 a11*10 b20 a11*7 b20 a11*6 b21*2 a20*6 b21 a20*11 b21 a20*5 b21 a20*13 b30
    a21*3 b30 a21*8 b30 a21*5 b30*2 a21*4 b30*2 a21*5 b30 a21*4 b30 a21 b30*3 a21*5 f10*5 b31 f10 b31 f10*2 b31
    f10*2 b31*2 f10*2 b31*2 f10*2 b31 f10*2 b31 f10*2 b31*3 f10 f11 b40 f11*7 b40 f11*11 b41*2
"""


def schedule():
    make = {"mha": mha_steps, "ffn": ffn_steps, "enter": enter_steps, "between": between_steps}
    kinds = {"e": "enter", "b": "between", "a": "mha", "f": "ffn"}
    order, live, plan = [], {}, []
    for word in ORDER.split():
        name, _, times = word.partition("*")
        order += [(kinds[name[0]], *map(int, name[1:]))] * int(times or 1)
    for key in order:
        if key not in live:
            live[key] = make[key[0]](*key[1:])
        for x in live[key]:
            if x == STEP:
                break
            plan.append(x)
    for rest in live.values():
        assert next(rest, None) is None
    return order, plan


FLAG = 3


class Signal:

    def __init__(self, sem, steps, inc=1, base=0):
        self.sem, self.steps, self.inc, self.base = sem, list(steps), inc, base
        self.at = {x: n for n, x in enumerate(self.steps)}

    def after(self, it, step):
        return it * (len(self.steps) * self.inc) + (self.base + (self.at[step] + 1) * self.inc)

    def before(self, it, step):
        return it * (len(self.steps) * self.inc) + (self.base + self.at[step] * self.inc)


def build(nc, t):
    order, plan = schedule()
    banks = [x for k, x in plan if k == "bank"]
    ys_, pvs = [x for k, x in plan if k == "acc"], [x for k, x in plan if k == "pv"]
    splits = [x for k, x in plan if k == "split"]
    rings = {kind: [x for k, x in plan if k == "ring" and x[0] == kind] for kind in "ht"}
    ring_size = {"h": H_RING, "t": T_RING}
    n_tiles = SLOTS * TILES
    lns = ["l0", "l1", "l2", "l3", "la", "lb", "l4", "l5"]
    links = [0]

    ctx = ExitStack()
    with ctx:
        def sb(name, shape, dt):
            return ctx.enter_context(nc.sbuf_tensor(name, shape, dt))

        def sem(name):
            return ctx.enter_context(nc.semaphore(name))

        w = sb("w", [P, 2, NW], F16)
        rb = sb("rb", [P, R_B2], F16)
        b2 = sb("b2", [P, D], F16)
        cb = sb("cb", [P, NC], F32)
        kc = sb("kc", [P, NK], F32)
        ident16 = sb("ident16", [P, P], F16)
        identb = sb("identb", [P, P], BF16)
        negsel = sb("negsel", [P, PAIRS, P], BF16)
        ones_rows = sb("ones_rows", [P, P], F16)
        half = sb("half", [P, TILES], F32)
        mk_bias = sb("mk_bias", [P, SLOTS, SEQS], F32)
        mk8 = sb("mk8", [P, SLOTS, SEQS], U8)
        seq_any = sb("seq_any", [P, SLOTS, SEQS], F32)
        xs = sb("xs", [P, SLOTS, TILES, D], F32)
        ys = sb("ys", [P, SLOTS, TILES, D], F32)
        os_ = ys[:].rearrange("p s t d -> p s (t d)")
        zs = sb("zs", [P, SLOTS, TILES, D], F32)
        qs = zs[:].rearrange("p s t d -> p s (t d)")
        xt = sb("xt", [P, SLOTS, 2, CHUNK], F16)
        ct = sb("ct", [P, SLOTS, 2, CHUNK], F16)
        qh = sb("qh", [P, SLOTS, 2, CHUNK], F16)
        kh = sb("kh", [P, SLOTS, 2, CHUNK], F16)
        oh = kh
        qstack = sb("qstack", [P, SLOTS, GROUPS, CHUNK], F16)
        kstack = sb("kstack", [P, SLOTS, 2, GROUPS * SEQS, 2, SEQ], F16)
        vm = sb("vm", [P, VRING, 2, 2, VW], F16)
        r32 = {kind: sb(f"r32_{kind}", [P, n, CHUNK], F32) for kind, n in ring_size.items()}
        rhl = {kind: sb(f"rhl_{kind}", [P, n, 2, CHUNK], F16) for kind, n in ring_size.items()}
        rden = sb("rden", [P, 2, 256], F32)
        mx = sb("mx", [P, SLOTS, TILES, HEADS], F32)
        mhl = sb("mhl", [P, 2, P], BF16)
        mt = sb("mt", [P, 2, P], BF16)
        amask = sb("amask", [P, SLOTS, CHUNK], BF16)
        kmask8 = sb("kmask8", [P, SLOTS, CHUNK], U8)
        stats = sb("stats", [P, SLOTS, TILES, 6], F32)
        mv = sb("mv", [P, SLOTS, TILES, 2], F32)
        ve = sb("ve", [P, SLOTS, TILES], F32)
        rstd = sb("rstd", [P, SLOTS, TILES], F32)
        sm = sb("sm", [P, SLOTS, 4, TILES], F32)
        gates = sb("gates", [P, SLOTS, TILES, E], F32)
        gw = sb("gw", [P, SLOTS, 12, TILES, E], F32)
        gm = sb("gm", [P, SLOTS, 8, TILES], F32)
        gstack = qstack[:, :, 0].rearrange("p s (t c) -> p s t c", t=TILES)
        gtr = qh[:, :, 0]
        psum = [ctx.enter_context(nc.psum_tensor(f"bank{i}", [P, CHUNK], F32)) for i in range(BANKS + Y_BANKS + PV_BANKS)]
        kd = [[nc.dram_tensor(f"k_scratch{m}{s}", [P, GROUPS, CHUNK], F16, kind="Internal").ap() for s in range(SLOTS)] for m in range(3)]

        in_stack = [kstack[:, s].rearrange("p v g u t -> p (v g u t)").bitcast(F32) for s in range(SLOTS)]
        in_ring = [r32["h"][:].rearrange("p r c -> p (r c)"), rhl["h"][:].rearrange("p r k c -> p (r k c)").bitcast(F32)]
        half_att = W_UP0 // 2
        part0, part1 = (W_GA1 - W_UP0) // 4, (NW - W_GA1) // 3
        pieces = [(n * half_att, half_att, in_ring[n][:, 0:half_att]) for n in range(2)]
        pieces += [(W_UP0 + n * part0, part0, in_stack[n // 2][:, n % 2 * part0:(n % 2 + 1) * part0]) for n in range(4)]
        pieces += [(W_GA1 + n * part1, part1, in_ring[n % 2][:, 0:part1]) for n in range(3)]
        ATTENTION_PIECES, MIXTURE0_PIECES, SPLIT_BY_TWO = 2, 6, 7
        biases_f32 = r32["t"][:].rearrange("p r c -> p (r c)")[:, 0:NR]
        consts_f32 = rhl["t"][:].rearrange("p r k c -> p (r k c)").bitcast(F32)[:, 0:NS]

        consts_in = sem("consts_in")
        stage_in = [sem(f"stage_in{i}") for i in range(len(pieces))]
        rot_done, w_hi, w_lo = sem("rot_done"), sem("w_hi"), sem("w_lo")
        small_prep, pool_prep, pool_split = sem("small_prep"), sem("pool_prep"), sem("pool_split")
        dve_link = sem("dve_link")
        pool_cleared = sem("pool_cleared")
        aggr_turn = sem("aggr_turn")
        prep_link = sem("prep_link")
        chunk_in = [Signal(sem(f"chunk_in{s}"), ["in"], 16) for s in range(SLOTS)]
        stored = [Signal(sem(f"stored{s}"), range(1), 16, base=1) for s in range(SLOTS)]
        home, all_read, first = {}, [], 0
        for steps, size in ((banks, BANKS), (ys_, Y_BANKS), (pvs, PV_BANKS)):
            for n in range(size):
                b, mine = first + n, steps[n::size]
                full, read = Signal(sem(f"bank_full{b}"), mine), Signal(sem(f"bank_read{b}"), mine, base=1)
                all_read.append(read)
                home.update({x: (psum[b], full, read) for x in mine})
            first += size
        hi = Signal(sem("split_hi"), splits)
        from_sbuf = [x for x in splits if x[0] in ("p", "mo") or x[:2] in (("q", 0), ("k", 0), ("mk", 0))]
        lo = Signal(sem("split_lo"), from_sbuf)
        r_hi = Signal(sem("hidden_hi"), [r for r in rings["h"] if r[1]])
        r_lo = {kind: Signal(sem(f"ring_lo_{kind}"), rings[kind]) for kind in "ht"}
        ends = {r: (("pv", r[1], r[2] // 2) if r[0] == "t" else ("y", r[1], r[2] // (D0, F1)[r[1]])) for r in rings["t"] + rings["h"]
                if (r[0] == "t" and r[2] % 2 and r[3]) or (r[0] == "h" and (r[2] + 1) % (D0, F1)[r[1]] == 0)}
        r_used = {kind: Signal(sem(f"ring_used_{kind}"), [r for r in rings[kind] if r not in ends]) for kind in "ht"}
        f32_ready = [Signal(sem(f"f32_ready{s}"), [("mk", 0), ("q", 0), ("k", 0), ("p", 0), ("mo", 0), ("p", 1), ("mo", 1), ("mo", 2)]) for s in range(SLOTS)]
        smax = [Signal(sem(f"softmax_max{s}"), range(2)) for s in range(SLOTS)]
        sexp = [Signal(sem(f"softmax_exp{s}"), range(2)) for s in range(SLOTS)]
        k_stored = [[Signal(sem(f"k_stored{m}{s}"), range(1), 64) for s in range(SLOTS)] for m in range(3)]
        k_in = [Signal(sem(f"k_stacked{s}"), range(3), 64) for s in range(SLOTS)]
        k_back = [Signal(sem(f"k_back{s}"), range(1), 32) for s in range(SLOTS)]
        zs_free = [Signal(sem(f"context_used{s}"), range(1), base=1) for s in range(SLOTS)]
        ctx_in = [Signal(sem(f"ctx_in{s}"), ["in"], 48) for s in range(SLOTS)]
        q_in = [Signal(sem(f"q_stacked{s}"), range(3), 64) for s in range(SLOTS)]
        halves3 = [(m, h) for m in range(3) for h in range(n_tiles // 2)]
        max_split = Signal(sem("max_split"), [(m, i) for m in range(3) for i in range(n_tiles)])
        v_hi = Signal(sem("v_hi"), [(m, i) for m in range(3) for i in range(n_tiles)])
        den_ln = Signal(sem("den_ln"), halves3)
        den_done = Signal(sem("den_reciprocal"), halves3)
        variance = [Signal(sem(f"variance{s}"), lns) for s in range(SLOTS)]
        rstd_done = [Signal(sem(f"rstd{s}"), lns) for s in range(SLOTS)]
        normed = [Signal(sem(f"normalised{s}"), lns[:2] + ["x1"] + lns[2:]) for s in range(SLOTS)]
        masks_ready = [Signal(sem(f"masks_ready{s}"), range(1)) for s in range(SLOTS)]
        gate_in = [Signal(sem(f"gate_shifted{s}"), range(2)) for s in range(SLOTS)]
        gate_exp = [Signal(sem(f"gate_exp{s}"), range(2)) for s in range(SLOTS)]
        gate_stack = [Signal(sem(f"gate_stack{s}"), range(1)) for s in range(SLOTS)]

        block = ctx.enter_context(nc.Block())

        def full_of(name):
            return home[name][1]

        def read_of(name):
            return home[name][2]

        def full_sem(name):
            return full_of(name).sem

        def full_value(it, name):
            return full_of(name).after(it, name)

        def read_sem(name):
            return read_of(name).sem

        def read_value(it, name):
            return read_of(name).after(it, name)

        def free_sem(name):
            return read_of(name).sem

        def free_value(it, name):
            return read_of(name).before(it, name)

        def split_sem(name):
            return lo.sem if name in lo.at else read_sem(name)

        def split_value(it, name):
            return lo.after(it, name) if name in lo.at else read_value(it, name)

        def used_sem(r):
            return full_sem(ends[r]) if r in ends else r_used[r[0]].sem

        def used_value(it, r):
            return full_value(it, ends[r]) if r in ends else r_used[r[0]].after(it, r)

        def place(r):
            return r_lo[r[0]].at[r] % ring_size[r[0]]

        def stood_there(r):
            n = r_lo[r[0]].at[r] - ring_size[r[0]]
            return rings[r[0]][n] if n >= 0 else None

        def link_value(it):
            links[0] += 1
            return it * LINKS + links[0]

        def bank_of(name):
            return home[name][0]

        def run(it, programs):
            live = {}
            for key in order:
                if key not in live:
                    live[key] = programs[key[0]](it, *key[1:])
                next(live[key])
            for program in live.values():
                assert next(program, "ended") == "ended"

        def flat(buf, s):
            return buf[:, s].rearrange("p t d -> p (t d)")

        def tiled(ap, n=TILES):
            return ap.rearrange("p (t d) -> p t d", t=n)

        def spread(ap, n):
            return ap.unsqueeze(2).broadcast_to([ap.shape[0], ap.shape[1], n])

        def repeat(ap, n):
            return ap.unsqueeze(1).broadcast_to([ap.shape[0], n, ap.shape[1]])

        def v_dst(i, k, p):
            return vm[64 * p:64 * p + 64, i % VRING, k, :, 32 * p:32 * p + PAIRS * (VSTEP + 1)].rearrange(
                "q s (j w) -> q s j w", j=PAIRS)[:, :, :, 0:4 * HD:4]

        def v_src(name, p):
            return bank_of(name)[64 * p:64 * p + 64, 0:128].rearrange("q (s j i) -> q s j i", s=2, i=HD)

        single_dst = {"v": qstack, "q": qh, "k": kh, "p": kh, "o": oh}

        @block.sync
        def _(sp):
            for n in range(ATTENTION_PIECES):
                o, c, staged = pieces[n]
                sp.dma_start(staged, t["weights"][:, o:o + c]).then_inc(stage_in[n], 16)
            sp.dma_start(kc[:], t["consts"]).then_inc(consts_in, 16)
            sp.dma_start(cb[:], t["col_bias"]).then_inc(consts_in, 16)
            sp.dma_start(consts_f32, t["consts16"]).then_inc(consts_in, 16)
            sp.dma_start(biases_f32, t["row_bias"]).then_inc(consts_in, 16)
            for s in range(SLOTS):
                sp.sem_inc(zs_free[s].sem, 1)
                sp.sem_inc(stored[s].sem, 1)
            with sp.Fori(0, ITERS) as it:
                for s in range(SLOTS):
                    base = it * (SLOTS * CHUNK) + s * CHUNK
                    sp.wait_ge(zs_free[s].sem, zs_free[s].before(it, 0))
                    sp.dma_start(zs[:, s], t["ctx"][bass.ds(base, CHUNK), :].rearrange("(t p) d -> p t d", p=P)).then_inc(ctx_in[s].sem, 16)
                    sp.dma_start(kmask8[:, s], t["mask_row"][:, bass.ds(base, CHUNK)].broadcast_to([P, CHUNK])).then_inc(ctx_in[s].sem, 16)
                    sp.dma_start(mk8[:, s], t["mask_cols"][:, bass.ds(it * (SLOTS * SEQS) + s * SEQS, SEQS)]).then_inc(ctx_in[s].sem, 16)
                for s in range(SLOTS):
                    base = it * (SLOTS * CHUNK) + s * CHUNK
                    sp.wait_ge(stored[s].sem, stored[s].before(it, 0))
                    sp.dma_start(xs[:, s], t["x"][bass.ds(base, CHUNK), :].rearrange("(t p) d -> p t d", p=P)).then_inc(chunk_in[s].sem, 16)

                def by_parts(scratch):
                    return scratch.rearrange("(ui a b) g t -> a b ui g t", a=2, b=2)

                def store_k(m, src, s):
                    for a in range(2):
                        for b in range(2):
                            sp.dma_start(by_parts(kd[m][s])[a, b], src[:, s, a]).then_inc(k_stored[m][s].sem, 16)

                def store_q(s):
                    for b in range(2):
                        for a in range(2):
                            sp.dma_start(qstack[2 * a + b:P:4, s], qh[:, s, b]).then_inc(q_in[s].sem, 16)

                def stack_k(m, s):
                    for u in range(4):
                        sp.dma_start(kstack[32 * u:32 * u + 32, s, u // 2, :, u % 2, :],
                                     kd[m][s][32 * u:32 * u + 32].rearrange("r g (s k) -> r (g s) k", k=SEQ)).then_inc(k_in[s].sem, 16)

                for s in range(SLOTS):
                    for m, src in ((0, kh), (2, qh)):
                        sp.wait_ge(split_sem(("mk", m, s)), split_value(it, ("mk", m, s)))
                        store_k(m, src, s)
                    sp.wait_ge(pool_prep, 1)
                    sp.wait_ge(k_stored[0][s].sem, k_stored[0][s].after(it, 0))
                    stack_k(0, s)
                for m in range(3):
                    for s in range(SLOTS):
                        if m == 1:
                            sp.wait_ge(split_sem(("mk", m, s)), split_value(it, ("mk", m, s)))
                            store_k(m, kh, s)
                        if m == 2:
                            name = ("t", 1, TILES * (s + 1) - 1, 1)
                            sp.wait_ge(full_sem(name), full_value(it, name))
                            sp.wait_ge(k_stored[2][s].sem, k_stored[2][s].after(it, 0))
                            stack_k(2, s)
                            sp.wait_ge(full_sem(("mw", 1, s)), full_value(it, ("mw", 1, s)))
                            for a in range(2):
                                sp.dma_start(kh[:, s, a], by_parts(kd[2][s])[a, 0]).then_inc(k_back[s].sem, 16)
                        sp.wait_ge(split_sem(("mq", m, s)), split_value(it, ("mq", m, s)))
                        store_q(s)
                        if m == 1:
                            sp.wait_ge(k_stored[1][s].sem, k_stored[1][s].after(it, 0))
                            stack_k(1, s)
            for s in range(SLOTS):
                sp.wait_ge(stored[s].sem, stored[s].before(ITERS, 0))

        @block.tensor
        def _(pe):
            mm = nc.tensor.matmul

            def prod3(out, left, right, first=True, last=True, check=False):
                mm(out, left(0), right(0), start=first, stop=False, skip_group_check=check)
                mm(out, left(0), right(1), start=False, stop=False, skip_group_check=check)
                return mm(out, left(1), right(0), start=False, stop=last, skip_group_check=check)

            def weight(col, n=D):
                return lambda k: w[:, k, col:col + n]

            def cols(buf, s, a, n):
                return lambda k: buf[:, s, k, a:a + n]

            def transposed(it, name, src, eye=K_ID):
                pe.wait_ge(free_sem(name), free_value(it, name))
                o = bank_of(name)
                for i in range(TILES):
                    last = nc.tensor.transpose(o[:, i * P:(i + 1) * P], src[:, i, :], kc[:, eye:eye + P])
                last.then_inc(full_sem(name), 1)

            def token_major(it, name, src, s, col, bias, n=D):
                pe.wait_ge(free_sem(name), free_value(it, name))
                o = bank_of(name)
                for i in range(TILES):
                    out = o[:, i * n:(i + 1) * n]
                    last = prod3(out, cols(src, s, i * P, P), weight(col, n), last=bias is None)
                    if bias is not None:
                        last = mm(out, ones_rows[:], rb[:, bias:bias + n], start=False, stop=True)
                last.then_inc(full_sem(name), 1)

            def feature_major(it, name, col, src, s):
                pe.wait_ge(free_sem(name), free_value(it, name))
                prod3(bank_of(name)[:], weight(col), lambda k: src[:, s, k]).then_inc(full_sem(name), 1)

            def input_t(it, name, src, after, s):
                pe.wait_ge(normed[s].sem, normed[s].after(it, after))
                transposed(it, ("T", name, s), src[:, s])
                yield

            def single(it, a, tname, s):
                pe.wait_ge(split_sem(("T", tname, s)), split_value(it, ("T", tname, s)))
                for x in "qk":
                    feature_major(it, (x, a, s), W_ONE[a, x] * D, xt, s)
                token_major(it, ("v", a, s), xt, s, W_ONE[a, "v"] * D, R_ONE[a, "v"] * D)
                yield
                pe.wait_ge(split_sem(("k", a, s)), split_value(it, ("k", a, s)))
                pe.wait_ge(free_sem(("s", a, s)), free_value(it, ("s", a, s)))
                o = bank_of(("s", a, s))
                for i in range(TILES):
                    last = prod3(o[:, i * P:(i + 1) * P], cols(qh, s, i * P, P), cols(kh, s, i * P, P))
                last.then_inc(full_sem(("s", a, s)), 1)
                yield
                yield
                yield
                pe.wait_ge(split_sem(("p", a, s)), split_value(it, ("p", a, s)))
                pe.wait_ge(free_sem(("pt", a, s)), free_value(it, ("pt", a, s)))
                o = bank_of(("pt", a, s))[:].bitcast(F16)
                for k in range(2):
                    for i in range(TILES):
                        c = k * CHUNK + i * P
                        last = nc.tensor.transpose(o[:, c:c + P], kh[:, s, k, i * P:(i + 1) * P], ident16[:])
                last.then_inc(full_sem(("pt", a, s)), 1)
                yield
                pe.wait_ge(read_sem(("pt", a, s)), read_value(it, ("pt", a, s)))
                pe.wait_ge(free_sem(("o", a, s)), free_value(it, ("o", a, s)))
                o = bank_of(("o", a, s))
                for i in range(TILES):
                    v, pt = cols(qstack, s, i * P, P), cols(qh, s, i * P, P)
                    last = prod3(o[:, i * P:(i + 1) * P], *((v, pt) if a else (pt, v)))
                last.then_inc(full_sem(("o", a, s)), 1)
                if a:
                    yield
                    pe.wait_ge(split_sem(("o", a, s)), split_value(it, ("o", a, s)))
                    token_major(it, ("wo", a, s), oh, s, W_ONE[a, "o"] * D, R_ONE[a, "o"] * D)
                yield

            def prepare(it, m, tname, s):
                pe.wait_ge(split_sem(("T", tname, s)), split_value(it, ("T", tname, s)))
                if m == 1:
                    feature_major(it, ("mk", m, s), W_MHA[m, "k"] * D, xt, s)
                feature_major(it, ("mq", m, s), W_MHA[m, "q"] * D, xt, s)
                yield

            def leave(it, m, s):
                if m == 2:
                    pe.wait_ge(f32_ready[s].sem, f32_ready[s].after(it, ("mo", m)))
                    transposed(it, ("ot", s), tiled(os_[:, s]), K_PERM)
                    yield
                    yield
                    yield from input_t(it, "o", zs, "la", s)
                else:
                    yield
                name = ("T", "o", s) if m == 2 else ("mo", m, s)
                pe.wait_ge(split_sem(name), split_value(it, name))
                token_major(it, ("mw", m, s), xt if m == 2 else oh, s, W_MHA[m, "o"] * D, R_MHA[m, "o"] * D)
                for _ in range(5 if m == 2 else 2):
                    yield

            def make_gates(it, f, tname, s):
                pe.wait_ge(split_sem(("T", tname, s)), split_value(it, ("T", tname, s)))
                token_major(it, ("g", f, s), xt, s, W_G1 if f else W_G0, None if f else R_G0, E)
                yield
                yield
                if f == 0:
                    pe.wait_ge(gate_stack[s].sem, gate_stack[s].after(it, 0))
                    pe.wait_ge(free_sem(("gt", s)), free_value(it, ("gt", s)))
                    o = bank_of(("gt", s))[:].bitcast(F16)
                    for i in range(TILES):
                        last = nc.tensor.transpose(o[:, i * P:(i + 1) * P], gstack[:, s, i, :], ident16[:])
                    last.then_inc(full_sem(("gt", s)), 1)
                    yield
                    pe.wait_ge(read_sem(("gt", s)), read_value(it, ("gt", s)))
                    pe.wait_ge(free_sem(("gb", s)), free_value(it, ("gb", s)))
                    o = bank_of(("gb", s))
                    for i in range(TILES):
                        last = mm(o[:, i * P:(i + 1) * P], gtr[:, s, i * P:(i + 1) * P], b2[:], start=True, stop=True)
                    last.then_inc(full_sem(("gb", s)), 1)
                yield

            def mha(it, m, s):
                src_kv = xt if m == 1 else ct

                def values_of(i):
                    s = i // TILES
                    src = kh if m == 2 else src_kv
                    if m == 2:
                        pe.wait_ge(k_back[s].sem, k_back[s].after(it, 0))
                    pe.wait_ge(free_sem(("mv", m, i)), free_value(it, ("mv", m, i)))
                    o = bank_of(("mv", m, i))
                    for b in range(2):
                        a0 = (i % TILES) * P + b * SEQ
                        for p in range(2):
                            out = o[64 * p:64 * p + 64, b * 64:(b + 1) * 64]
                            prod3(out, cols(src, s, a0, SEQ), weight(W_MHA[m, "v"] * D + 64 * p, 64), last=False)
                            c = R_MHA[m, "v"] * D + 64 * p
                            last = mm(out, ones_rows[:, 0:SEQ], rb[:, c:c + 64], start=False, stop=True)
                    last.then_inc(full_sem(("mv", m, i)), 1)

                def scores(i):
                    s = i // TILES
                    if i % TILES == 0:
                        pe.wait_ge(k_in[s].sem, k_in[s].after(it, m))
                        pe.wait_ge(q_in[s].sem, q_in[s].after(it, m))
                        if m == 0:
                            pe.wait_ge(masks_ready[s].sem, masks_ready[s].after(it, 0))
                    for hb in range(2):
                        pe.wait_ge(free_sem(("n", m, i, hb)), free_value(it, ("n", m, i, hb)))
                        o = bank_of(("n", m, i, hb))
                        for gi in range(2):
                            for b in range(2):
                                c0 = (i % TILES) * P + b * SEQ
                                g = 2 * hb + gi
                                keys = kstack[:, s, :, g * SEQS + c0 // SEQ].rearrange("p v u k -> p v (u k)")
                                out = o[b * SEQ:(b + 1) * SEQ, gi * 256:(gi + 1) * 256]
                                last = mm(out, qstack[:, s, g, c0:c0 + SEQ], keys, start=True, stop=m > 0)
                                if m == 0:
                                    last = mm(out, ones_rows[:, 0:SEQ], repeat(amask[:, s, c0:c0 + SEQ], 4), start=False, stop=True)
                        last.then_inc(full_sem(("n", m, i, hb)), 1)

                def maxima_t(i):
                    pe.wait_ge(max_split.sem, max_split.after(it, (m, i)))
                    pe.wait_ge(free_sem(("mt", m, i)), free_value(it, ("mt", m, i)))
                    o = bank_of(("mt", m, i))[:].bitcast(BF16)
                    nc.tensor.transpose(o[:, 0:P], mhl[:, i % 2, :], identb[:]).then_inc(full_sem(("mt", m, i)), 1)

                def scores_t(i, b):
                    s = i // TILES
                    if b == 0:
                        pe.wait_ge(read_sem(("mt", m, i)), read_value(it, ("mt", m, i)))
                    c0 = (i % TILES) * P + b * SEQ
                    pe.wait_ge(free_sem(("t", m, i, b)), free_value(it, ("t", m, i, b)))
                    o = bank_of(("t", m, i, b))
                    for j in range(PAIRS):
                        vp, g = j // 4, j % 4
                        out = o[:, j * SEQ:(j + 1) * SEQ]
                        mm(out, kstack[:, s, vp, g * SEQS + c0 // SEQ].rearrange("p u k -> p (u k)"), qstack[:, s, g, c0:c0 + SEQ], start=True, stop=False)
                        last = mm(out, negsel[:, j, :], mt[:, i % 2, b * SEQ:(b + 1) * SEQ], start=False, stop=True)
                    last.then_inc(full_sem(("t", m, i, b)), 1)

                def attend(i):
                    h = i // 2
                    name = ("pv", m, h)
                    if i % 2 == 0:
                        pe.wait_ge(free_sem(name), free_value(it, name))
                    pe.wait_ge(read_sem(("mv", m, i)), read_value(it, ("mv", m, i)))
                    o = bank_of(name)
                    for b in range(2):
                        r = ("t", m, i, b)
                        pe.wait_ge(r_lo["t"].sem, r_lo["t"].after(it, r))
                        ri = place(r)
                        sq = 2 * (i % 2) + b
                        for vp in range(2):
                            out = o[:, vp * 256 + sq * SEQ:vp * 256 + (sq + 1) * SEQ]
                            for g in range(4):
                                j = 4 * vp + g
                                c = VSTEP * j - VBACK * vp
                                last = prod3(out, lambda k: vm[:, i % VRING, k, b, c:c + P],
                                             lambda k: rhl["t"][:, ri, k, j * SEQ:(j + 1) * SEQ], first=g == 0, last=g == 3)
                        if b == 0:
                            last.then_inc(r_used["t"].sem, 1)
                    if i % 2 == 1:
                        last.then_inc(full_sem(name), 1)
                    else:
                        last.then_inc(r_used["t"].sem, 1)

                for n in range(TILES + 3):
                    i = s * TILES + n
                    if n < TILES:
                        scores(i)
                    yield
                    if n < VRING:
                        values_of(i)
                    if 1 <= n <= TILES:
                        maxima_t(i - 1)
                    yield
                    for b in range(2):
                        if 2 <= n < TILES + 2:
                            scores_t(i - 2, b)
                        yield
                    if n >= 3:
                        attend(i - 3)
                        if n - 3 + VRING < TILES:
                            values_of(i - 3 + VRING)
                    yield

            def ffn(it, f, s):
                inner = (D0, F1)[f]
                total = E * inner
                up, down = (W_UP0, W_UP1)[f], (W_DN0, W_DN1)[f]
                pe.wait_ge(w_lo, SPLIT_BY_TWO if f else MIXTURE0_PIECES)
                if f:
                    pe.wait_ge(pool_split, 2 * (len(pieces) - SPLIT_BY_TWO))
                for n in range(total + FLAG):
                    i = s * total + n
                    if n < total:
                        if f == 1:
                            feature_major(it, ("ga", f, i), W_GA1 + n * D, xt, s)
                        feature_major(it, ("up", f, i), up + n * D, xt, s)
                    if n >= FLAG:
                        q, c = i - FLAG, n - FLAG
                        name = ("y", f, q // inner)
                        if c % inner == 0:
                            pe.wait_ge(free_sem(name), free_value(it, name))
                        o = bank_of(name)
                        r = ("h", f, q)
                        pe.wait_ge(r_lo["h"].sem, r_lo["h"].after(it, r))
                        ri = place(r)
                        for ti in range(TILES):
                            last = prod3(o[:, ti * P:(ti + 1) * P], lambda k: rhl["h"][:, ri, k, ti * P:(ti + 1) * P], weight(down + c * D),
                                         first=c % inner == 0 and ti == 0, last=c % inner == inner - 1, check=True)
                        if c % inner == inner - 1:
                            last.then_inc(full_sem(name), 1)
                        else:
                            last.then_inc(r_used["h"].sem, 1)
                    yield

            def enter(it, s):
                pe.wait_ge(ctx_in[s].sem, ctx_in[s].after(it, "in"))
                transposed(it, ("T", "c", s), zs[:, s])
                yield
                pe.wait_ge(split_sem(("T", "c", s)), split_value(it, ("T", "c", s)))
                for m in (0, 2):
                    feature_major(it, ("mk", m, s), W_MHA[m, "k"] * D, ct, s)
                yield
                pe.wait_ge(chunk_in[s].sem, chunk_in[s].after(it, "in"))
                transposed(it, ("T", "x0", s), xs[:, s])
                yield
                yield from single(it, 0, "x0", s)
                yield
                yield from input_t(it, "x1", xs, "l0", s)
                yield from prepare(it, 0, "x1", s)

            def between(it, k, s):
                if k == 0:
                    yield from leave(it, 0, s)
                    yield from input_t(it, "x2", xs, "l1", s)
                    yield from single(it, 1, "x2", s)
                    yield from input_t(it, "x3", zs, "x1", s)
                    yield from make_gates(it, 0, "x3", s)
                elif k == 1:
                    yield
                    yield
                    yield from input_t(it, "x4", xs, "l2", s)
                    yield from prepare(it, 1, "x4", s)
                elif k == 2:
                    yield from leave(it, 1, s)
                    yield from input_t(it, "x5", xs, "l3", s)
                    yield from prepare(it, 2, "x5", s)
                elif k == 3:
                    yield from leave(it, 2, s)
                    yield from input_t(it, "x6", xs, "l4", s)
                    yield from make_gates(it, 1, "x6", s)
                else:
                    yield
                    yield

            pe.wait_ge(small_prep, 1)
            pe.wait_ge(w_lo, ATTENTION_PIECES)
            with pe.Fori(0, ITERS) as it:
                run(it, {"enter": enter, "between": between, "mha": mha, "ffn": ffn})

        @block.scalar
        def _(act):
            go = nc.scalar.activation

            def split_hi(it, name, dst, bias=None, f32=None):
                if f32 is None:
                    act.wait_ge(full_sem(name), full_value(it, name))
                    f32 = bank_of(name)[:]
                if bias is None:
                    go(dst, f32, ACT.Copy).then_inc(hi.sem, 1)
                else:
                    go(dst, f32, ACT.Identity, bias=cb[:, bias:bias + 1]).then_inc(hi.sem, 1)

            def transposed_hi(it, name, dst, s):
                split_hi(it, ("T", name, s), dst[:, s, 0])
                yield

            def single(it, a, s):
                split_hi(it, ("v", a, s), qstack[:, s, 0])
                for x, dst, f32 in (("q", qh, qs), ("k", kh, os_)):
                    if a == 0:
                        act.wait_ge(f32_ready[s].sem, f32_ready[s].after(it, (x, 0)))
                        stacked = k_stored[2 if x == "q" else 0][s]
                        act.wait_ge(stacked.sem, stacked.after(it, 0))
                        split_hi(it, (x, a, s), dst[:, s, 0], f32=f32[:, s])
                    else:
                        split_hi(it, (x, a, s), dst[:, s, 0], bias=C_ONE[a, x])
                yield
                act.wait_ge(smax[s].sem, smax[s].after(it, a))
                for i in range(TILES):
                    tile = os_[:, s, i * P:(i + 1) * P]
                    last = go(tile, tile, ACT.Exp, bias=sm[:, s, 1, i:i + 1], scale=ONE_SCALE[a], accum_out=sm[:, s, 2, i:i + 1])
                last.then_inc(sexp[s].sem, 1)
                yield
                act.wait_ge(f32_ready[s].sem, f32_ready[s].after(it, ("p", a)))
                split_hi(it, ("p", a, s), kh[:, s, 0], f32=os_[:, s])
                yield
                yield
                name = ("pt", a, s)
                act.wait_ge(full_sem(name), full_value(it, name))
                go(qh[:, s].rearrange("p k t -> p (k t)"), bank_of(name)[:].bitcast(F16), ACT.Copy).then_inc(read_sem(name), 1)
                yield
                if a:
                    split_hi(it, ("o", a, s), oh[:, s, 0])
                    yield
                yield

            def prepare(it, m, s):
                if m == 1:
                    split_hi(it, ("mk", m, s), kh[:, s, 0], bias=C_MHA[m, "k"])
                if m == 2:
                    act.wait_ge(full_sem(("mq", m, s)), full_value(it, ("mq", m, s)))
                    c = C_MHA[m, "q"]
                    go(qs[:, s], bank_of(("mq", m, s))[:], ACT.Identity, bias=cb[:, c:c + 1])
                split_hi(it, ("mq", m, s), qh[:, s, 0], bias=C_MHA[m, "q"])
                yield

            def leave(it, m, s):
                if m < 2:
                    act.wait_ge(f32_ready[s].sem, f32_ready[s].after(it, ("mo", m)))
                    split_hi(it, ("mo", m, s), oh[:, s, 0], f32=os_[:, s])
                    yield
                    yield
                    yield
                    return
                act.wait_ge(full_sem(("ot", s)), full_value(it, ("ot", s)))
                go(flat(ys, s), bank_of(("ot", s))[:], ACT.Copy).then_inc(read_sem(("ot", s)), 1)
                yield
                yield
                yield from transposed_hi(it, "o", xt, s)
                name = ("mw", m, s)
                act.wait_ge(full_sem(name), full_value(it, name))
                go(flat(ys, s), bank_of(name)[:], ACT.Gelu).then_inc(read_sem(name), 1)
                nc.scalar.preload_act_table_set(EXP_LN)
                for _ in range(5):
                    yield

            def make_gates(it, f, s):
                act.wait_ge(gate_in[s].sem, gate_in[s].after(it, f))
                if f == 0:
                    go(gw[:, s, 1], gw[:, s, 0], ACT.Exp).then_inc(gate_exp[s].sem, 1)
                else:
                    go(gw[:, s, 2:4], gw[:, s, 0:2], ACT.Exp, scale=-1.0).then_inc(gate_exp[s].sem, 1)
                yield
                yield
                if f == 0:
                    name = ("gt", s)
                    act.wait_ge(full_sem(name), full_value(it, name))
                    go(gtr[:, s], bank_of(name)[:].bitcast(F16)[:, 0:CHUNK], ACT.Copy).then_inc(read_sem(name), 1)
                    yield
                yield

            def mha(it, m, s):
                def place_v(i):
                    name = ("mv", m, i)
                    act.wait_ge(full_sem(name), full_value(it, name))
                    old = (m, i - VRING) if i >= VRING else (m - 1, n_tiles + i - VRING)
                    if old[0] >= 0:
                        act.wait_ge(used_sem(("t", *old, 1)), used_value(it, ("t", *old, 1)))
                    for p in range(2):
                        last = go(v_dst(i, 0, p), v_src(name, p), ACT.Copy)
                    last.then_inc(v_hi.sem, 1)

                for n in range(TILES + 3):
                    i = s * TILES + n
                    yield
                    if n < VRING:
                        place_v(i)
                    if 1 <= n <= TILES:
                        q = i - 1
                        name = ("mt", m, q)
                        act.wait_ge(full_sem(name), full_value(it, name))
                        if q >= 2:
                            act.wait_ge(full_sem(("t", m, q - 2, 1)), full_value(it, ("t", m, q - 2, 1)))
                        go(mt[:, q % 2, :], bank_of(name)[:].bitcast(BF16)[:, 0:P], ACT.Copy).then_inc(read_sem(name), 1)
                    yield
                    for b in range(2):
                        if 2 <= n < TILES + 2:
                            name = ("t", m, i - 2, b)
                            ri, old = place(name), stood_there(name)
                            act.wait_ge(full_sem(name), full_value(it, name))
                            if old is not None:
                                act.wait_ge(r_lo["t"].sem, r_lo["t"].after(it, old))
                                act.wait_ge(used_sem(old), used_value(it, old))
                            sq = 2 * (n - 2) + b
                            bias = {"bias": mk_bias[:, s, sq:sq + 1]} if m == 0 else {}
                            go(r32["t"][:, ri, :], bank_of(name)[:], ACT.Exp, scale=MHA_SCALE, **bias)
                            go(rhl["t"][:, ri, 0, :], bank_of(name)[:], ACT.Exp, scale=MHA_SCALE, **bias).then_inc(read_sem(name), 1)
                        yield
                    if n >= 3 and n - 3 + VRING < TILES:
                        place_v(i - 3 + VRING)
                    if n >= 3 and (n - 3) % 2 == 1:
                        h = (i - 3) // 2
                        name = ("pv", m, h)
                        act.wait_ge(full_sem(name), full_value(it, name))
                        o = bank_of(name)
                        go(rden[0:64, h % 2, :], o[64:128, 0:256], ACT.Ln)
                        go(rden[64:128, h % 2, :], o[0:64, 256:512], ACT.Ln).then_inc(den_ln.sem, 1)
                        act.wait_ge(den_ln.sem, den_ln.after(it, (m, h)))
                        go(rden[:, h % 2, :], rden[:, h % 2, :], ACT.Exp, scale=-1.0).then_inc(den_done.sem, 1)
                    yield

            def ffn(it, f, s):
                total = E * (D0, F1)[f]
                for n in range(total + FLAG):
                    i = s * total + n
                    if n < total:
                        r = ("h", f, i)
                        f32, old = r32["h"][:, place(r), :], stood_there(r)
                        name = ("ga" if f else "up", f, i)
                        act.wait_ge(full_sem(name), full_value(it, name))
                        if old is not None:
                            act.wait_ge(r_lo["h"].sem, r_lo["h"].after(it, old))
                        if f == 0:
                            c = C_B1 + n
                            if old is not None:
                                act.wait_ge(used_sem(old), used_value(it, old))
                            go(f32, bank_of(name)[:], ACT.Relu, bias=cb[:, c:c + 1])
                            go(rhl["h"][:, place(r), 0, :], bank_of(name)[:], ACT.Relu, bias=cb[:, c:c + 1]).then_inc(read_sem(name), 1)
                        else:
                            go(f32, bank_of(name)[:], ACT.Silu).then_inc(read_sem(name), 1)
                    if f == 1 and 1 <= n <= total:
                        r = ("h", f, i - 1)
                        old = stood_there(r)
                        act.wait_ge(read_sem(("up", f, i - 1)), read_value(it, ("up", f, i - 1)))
                        act.wait_ge(used_sem(old), used_value(it, old))
                        go(rhl["h"][:, place(r), 0, :], r32["h"][:, place(r), :], ACT.Copy).then_inc(r_hi.sem, 1)
                    yield

            def enter(it, s):
                yield from transposed_hi(it, "c", ct, s)
                act.wait_ge(f32_ready[s].sem, f32_ready[s].after(it, ("mk", 0)))
                split_hi(it, ("mk", 0, s), kh[:, s, 0], f32=qs[:, s])
                split_hi(it, ("mk", 2, s), qh[:, s, 0], bias=C_MHA[2, "k"])
                yield
                yield from transposed_hi(it, "x0", xt, s)
                yield from single(it, 0, s)
                yield
                yield from transposed_hi(it, "x1", xt, s)
                yield from prepare(it, 0, s)

            def between(it, k, s):
                if k == 0:
                    yield from leave(it, 0, s)
                    yield from transposed_hi(it, "x2", xt, s)
                    yield from single(it, 1, s)
                    yield from transposed_hi(it, "x3", xt, s)
                    yield from make_gates(it, 0, s)
                elif k == 1:
                    yield
                    yield
                    yield from transposed_hi(it, "x4", xt, s)
                    yield from prepare(it, 1, s)
                elif k == 2:
                    yield from leave(it, 1, s)
                    yield from transposed_hi(it, "x5", xt, s)
                    yield from prepare(it, 2, s)
                elif k == 3:
                    yield from leave(it, 2, s)
                    yield from transposed_hi(it, "x6", xt, s)
                    yield from make_gates(it, 1, s)
                else:
                    yield
                    base = it * (SLOTS * CHUNK) + s * CHUNK
                    act.wait_ge(normed[s].sem, normed[s].after(it, "l5"))
                    act.dma_start(t["out"][bass.ds(base, CHUNK), :].rearrange("(t p) d -> p t d", p=P), xs[:, s]).then_inc(stored[s].sem, 16)
                    yield

            for n, (o, c, staged) in enumerate(pieces[:SPLIT_BY_TWO]):
                act.wait_ge(stage_in[n], 16)
                if n == 0:
                    act.wait_ge(rot_done, 1)
                go(w[:, 0, o:o + c], staged, ACT.Copy).then_inc(w_hi, 1)
            act.wait_ge(pool_cleared, 3)
            with act.Fori(0, ITERS) as it:
                nc.scalar.preload_act_table_set(EXP_LN)
                run(it, {"enter": enter, "between": between, "mha": mha, "ffn": ffn})

        @block.vector
        def _(dve):
            v = nc.vector

            def split_lo(it, name, dst, bias=None, f32=None):
                dve.wait_ge(hi.sem, hi.after(it, name))
                if f32 is not None:
                    v.tensor_tensor(dst[:, 1], f32, dst[:, 0], ALU.subtract).then_inc(lo.sem, 1)
                elif bias is None:
                    v.tensor_tensor(dst[:, 1], bank_of(name)[:], dst[:, 0], ALU.subtract).then_inc(read_sem(name), 1)
                else:
                    v.scalar_tensor_tensor(dst[:, 1], bank_of(name)[:], cb[:, bias:bias + 1], dst[:, 0], ALU.add, ALU.subtract).then_inc(read_sem(name), 1)

            def transposed_lo(it, name, dst, s):
                split_lo(it, ("T", name, s), dst[:, s])
                yield

            def norm_stats(it, name, s, src):
                for i in range(TILES):
                    last = v.bn_stats(stats[:, s, i, :], src[:, s, i, :])
                last.then_inc(dve_link, 1)
                dve.wait_ge(dve_link, link_value(it))
                dve.sem_inc(aggr_turn, 1)
                for i in range(TILES):
                    last = v.bn_aggr(mv[:, s, i, :], stats[:, s, i, :])
                last.then_inc(dve_link, 1)
                dve.wait_ge(dve_link, link_value(it))
                v.tensor_scalar(ve[:, s, :], mv[:, s, :, 1], EPS, None, ALU.add).then_inc(variance[s].sem, 1)

            def norm_apply(it, name, s, src, dst, affine=None):
                dve.wait_ge(rstd_done[s].sem, rstd_done[s].after(it, name))
                for i in range(TILES):
                    last = v.tensor_scalar(dst[:, s, i, :], src[:, s, i, :], mv[:, s, i, 0:1], rstd[:, s, i:i + 1], ALU.subtract, ALU.mult)
                if affine is not None:
                    c = K_LN + affine * D
                    last.then_inc(dve_link, 1)
                    dve.wait_ge(dve_link, link_value(it))
                    v.tensor_tensor(dst[:, s], dst[:, s], repeat(kc[:, c:c + D], TILES), ALU.mult).then_inc(dve_link, 1)
                    dve.wait_ge(dve_link, link_value(it))
                    last = v.tensor_tensor(dst[:, s], dst[:, s], repeat(kc[:, c + D:c + 2 * D], TILES), ALU.add)
                last.then_inc(normed[s].sem, 1)

            def residual_norm(it, name, step, s):
                step = (*step, s)
                dve.wait_ge(full_sem(step), full_value(it, step))
                v.tensor_tensor(flat(ys, s), bank_of(step)[:], flat(xs, s), ALU.add).then_inc(read_sem(step), 1)
                dve.wait_ge(read_sem(step), read_value(it, step))
                norm_stats(it, name, s, ys)
                yield
                norm_apply(it, name, s, ys, xs)
                yield

            def single(it, a, s):
                if a == 0:
                    for x, dst in (("q", qs), ("k", os_)):
                        dve.wait_ge(full_sem((x, 0, s)), full_value(it, (x, 0, s)))
                        c = C_ONE[0, x]
                        v.scalar_tensor_tensor(tiled(dst[:, s], SEQS), tiled(bank_of((x, 0, s))[:], SEQS), cb[:, c:c + 1],
                                               repeat(kc[:, K_ROPE:K_ROPE + SEQ], SEQS), ALU.add, ALU.mult).then_inc(read_sem((x, 0, s)), 1)
                        dve.wait_ge(read_sem((x, 0, s)), read_value(it, (x, 0, s)))
                        dve.sem_inc(f32_ready[s].sem, 1)
                split_lo(it, ("v", a, s), qstack[:, s])
                for x, dst, f32 in (("q", qh, qs), ("k", kh, os_)):
                    if a == 0:
                        split_lo(it, (x, a, s), dst[:, s], f32=f32[:, s])
                    else:
                        split_lo(it, (x, a, s), dst[:, s], bias=C_ONE[a, x])
                yield
                name = ("s", a, s)
                dve.wait_ge(full_sem(name), full_value(it, name))
                if a == 0:
                    dve.wait_ge(split_sem(("k", a, s)), split_value(it, ("k", a, s)))
                v.tensor_tensor(tiled(os_[:, s]), tiled(bank_of(name)[:]), repeat(kc[:, K_CROSS:K_CROSS + P], TILES), ALU.add).then_inc(read_sem(name), 1)
                dve.wait_ge(read_sem(name), read_value(it, name))
                v.reduce_max(sm[:, s, 0, :], tiled(os_[:, s]), AX).then_inc(dve_link, 1)
                dve.wait_ge(dve_link, link_value(it))
                v.tensor_scalar(sm[:, s, 1, :], sm[:, s, 0, :], -ONE_SCALE[a], None, ALU.mult).then_inc(smax[s].sem, 1)
                yield
                dve.wait_ge(sexp[s].sem, sexp[s].after(it, a))
                v.reciprocal(sm[:, s, 3, :], sm[:, s, 2, :]).then_inc(dve_link, 1)
                dve.wait_ge(dve_link, link_value(it))
                v.tensor_tensor(tiled(os_[:, s]), tiled(os_[:, s]), spread(sm[:, s, 3, :], P), ALU.mult).then_inc(f32_ready[s].sem, 1)
                yield
                split_lo(it, ("p", a, s), kh[:, s], f32=os_[:, s])
                yield
                yield
                if a == 0:
                    yield from residual_norm(it, "l0", ("o", 0), s)
                else:
                    split_lo(it, ("o", a, s), oh[:, s])
                    yield
                    name = ("wo", a, s)
                    dve.wait_ge(full_sem(name), full_value(it, name))
                    v.tensor_tensor(flat(zs, s), bank_of(name)[:], flat(xs, s), ALU.add).then_inc(read_sem(name), 1)
                    dve.wait_ge(read_sem(name), read_value(it, name))
                    dve.sem_inc(normed[s].sem, 1)
                    yield

            def masks(it, s):
                v.tensor_copy(os_[:, s], kmask8[:, s]).then_inc(dve_link, 1)
                dve.wait_ge(dve_link, link_value(it))
                v.reduce_max(seq_any[:, s], tiled(os_[:, s], SEQS), AX).then_inc(dve_link, 1)
                dve.wait_ge(dve_link, link_value(it))
                v.tensor_tensor(tiled(os_[:, s], SEQS), tiled(os_[:, s], SEQS), spread(seq_any[:, s], SEQ), ALU.subtract).then_inc(dve_link, 1)
                dve.wait_ge(dve_link, link_value(it))
                v.tensor_scalar(amask[:, s], os_[:, s], -MASKED / MHA_SCALE, None, ALU.mult)
                v.tensor_tensor(mk_bias[:, s], mk8[:, s], seq_any[:, s], ALU.subtract).then_inc(dve_link, 1)
                dve.wait_ge(dve_link, link_value(it))
                v.tensor_scalar(mk_bias[:, s], mk_bias[:, s], -MASKED, None, ALU.mult).then_inc(masks_ready[s].sem, 1)

            def context_keys(it, s):
                name = ("mk", 0, s)
                dve.wait_ge(ctx_in[s].sem, ctx_in[s].after(it, "in"))
                dve.wait_ge(full_sem(name), full_value(it, name))
                c = C_MHA[0, "k"]
                v.scalar_tensor_tensor(qs[:, s], bank_of(name)[:], cb[:, c:c + 1], kmask8[:, s], ALU.add, ALU.mult).then_inc(read_sem(name), 1)
                dve.wait_ge(read_sem(name), read_value(it, name))
                dve.sem_inc(f32_ready[s].sem, 1)
                split_lo(it, name, kh[:, s], f32=qs[:, s])
                split_lo(it, ("mk", 2, s), qh[:, s], bias=C_MHA[2, "k"])
                yield

            def prepare(it, m, s):
                if m == 1:
                    split_lo(it, ("mk", m, s), kh[:, s], bias=C_MHA[m, "k"])
                split_lo(it, ("mq", m, s), qh[:, s], bias=C_MHA[m, "q"])
                yield

            def leave(it, m, s):
                if m < 2:
                    split_lo(it, ("mo", m, s), oh[:, s], f32=os_[:, s])
                    yield
                    yield from residual_norm(it, ("l1", "l3")[m], ("mw", m), s)
                    return
                dve.wait_ge(read_sem(("ot", s)), read_value(it, ("ot", s)))
                norm_stats(it, "la", s, ys)
                yield
                norm_apply(it, "la", s, ys, zs, 0)
                yield
                yield from transposed_lo(it, "o", xt, s)
                yield
                dve.wait_ge(read_sem(("mw", m, s)), read_value(it, ("mw", m, s)))
                v.tensor_tensor(flat(ys, s), flat(ys, s), flat(zs, s), ALU.add).then_inc(dve_link, 1)
                dve.wait_ge(dve_link, link_value(it))
                norm_stats(it, "lb", s, ys)
                yield
                norm_apply(it, "lb", s, ys, zs, 2)
                yield
                dve.wait_ge(normed[s].sem, normed[s].after(it, "lb"))
                v.tensor_tensor(flat(ys, s), flat(zs, s), flat(xs, s), ALU.add).then_inc(dve_link, 1)
                dve.wait_ge(dve_link, link_value(it))
                dve.sem_inc(zs_free[s].sem, 1)
                norm_stats(it, "l4", s, ys)
                yield
                norm_apply(it, "l4", s, ys, xs)
                yield

            def mha(it, m, s):
                def place_v(i):
                    name = ("mv", m, i)
                    dve.wait_ge(v_hi.sem, v_hi.after(it, (m, i)))
                    for p in range(2):
                        last = v.tensor_tensor(v_dst(i, 1, p), v_src(name, p), v_dst(i, 0, p), ALU.subtract)
                    last.then_inc(read_sem(name), 1)

                def maxima(i):
                    s, ti = i // TILES, i % TILES
                    for hb in range(2):
                        name = ("n", m, i, hb)
                        dve.wait_ge(full_sem(name), full_value(it, name))
                        v.reduce_max(mx[:, s, ti, 8 * hb:8 * hb + 8], tiled(bank_of(name)[:], 8), AX).then_inc(read_sem(name), 1)
                    dve.wait_ge(read_sem(("n", m, i, 1)), read_value(it, ("n", m, i, 1)))
                    if i >= 2:
                        dve.wait_ge(full_sem(("mt", m, i - 2)), full_value(it, ("mt", m, i - 2)))
                    v.tensor_copy(mhl[:, i % 2, 0:HEADS], mx[:, s, ti, :]).then_inc(dve_link, 1)
                    dve.wait_ge(dve_link, link_value(it))
                    v.tensor_tensor(mhl[:, i % 2, HEADS:2 * HEADS], mx[:, s, ti, :], mhl[:, i % 2, 0:HEADS], ALU.subtract).then_inc(max_split.sem, 1)

                for n in range(TILES + 3):
                    i = s * TILES + n
                    if n < TILES:
                        maxima(i)
                    yield
                    if n < VRING:
                        place_v(i)
                    yield
                    yield
                    yield
                    if n >= 3 and n - 3 + VRING < TILES:
                        place_v(i - 3 + VRING)
                    if n >= 3 and (n - 3) % 2 == 1:
                        h = (i - 3) // 2
                        name = ("pv", m, h)
                        dve.wait_ge(den_done.sem, den_done.after(it, (m, h)))
                        o, c = bank_of(name), (h % 2) * 256
                        v.tensor_tensor(os_[0:64, s, c:c + 256], o[0:64, 0:256], rden[0:64, h % 2, :], ALU.mult)
                        v.tensor_tensor(os_[64:128, s, c:c + 256], o[64:128, 256:512], rden[64:128, h % 2, :], ALU.mult).then_inc(read_sem(name), 1)
                        if h % 2 == 1:
                            dve.wait_ge(read_sem(name), read_value(it, name))
                            if m == 2:
                                v.tensor_tensor(os_[:, s], os_[:, s], qs[:, s], ALU.add).then_inc(f32_ready[s].sem, 1)
                            else:
                                dve.sem_inc(f32_ready[s].sem, 1)
                    yield

            def gates_dense(it, s):
                name = ("g", 0, s)
                dve.wait_ge(full_sem(name), full_value(it, name))
                lg = bank_of(name)[:, 0:TILES * E].rearrange("p (t e) -> p t e", e=E)
                v.reduce_max(gm[:, s, 0], lg, AX).then_inc(dve_link, 1)
                dve.wait_ge(dve_link, link_value(it))
                v.tensor_tensor(gw[:, s, 0], lg, spread(gm[:, s, 0], E), ALU.subtract).then_inc(read_sem(name), 1)
                dve.wait_ge(read_sem(name), read_value(it, name))
                dve.sem_inc(gate_in[s].sem, 1)
                yield
                dve.wait_ge(gate_exp[s].sem, gate_exp[s].after(it, 0))
                v.reduce_sum(gm[:, s, 1], gw[:, s, 1], AX).then_inc(dve_link, 1)
                dve.wait_ge(dve_link, link_value(it))
                v.reciprocal(gm[:, s, 2], gm[:, s, 1]).then_inc(dve_link, 1)
                dve.wait_ge(dve_link, link_value(it))
                v.tensor_tensor(gates[:, s], gw[:, s, 1], spread(gm[:, s, 2], E), ALU.mult).then_inc(dve_link, 1)
                dve.wait_ge(dve_link, link_value(it))
                v.memset(gstack[:, s], 0.0).then_inc(dve_link, 1)
                dve.wait_ge(dve_link, link_value(it))
                v.tensor_copy(gstack[:, s, :, 64:64 + E], gates[:, s])
                v.tensor_copy(gstack[:, s, :, 0:E], gates[:, s]).then_inc(dve_link, 1)
                dve.wait_ge(dve_link, link_value(it))
                v.tensor_tensor(gstack[:, s, :, 32:32 + E], gates[:, s], gstack[:, s, :, 0:E], ALU.subtract).then_inc(gate_stack[s].sem, 1)
                yield
                yield
                name = ("gb", s)
                dve.wait_ge(full_sem(name), full_value(it, name))
                v.tensor_tensor(flat(ys, s), bank_of(name)[:], flat(zs, s), ALU.add).then_inc(read_sem(name), 1)
                dve.wait_ge(read_sem(name), read_value(it, name))
                v.tensor_tensor(flat(ys, s), flat(ys, s), flat(xs, s), ALU.add).then_inc(dve_link, 1)
                dve.wait_ge(dve_link, link_value(it))
                yield

            def gates_top2(it, s):
                name = ("g", 1, s)
                dve.wait_ge(full_sem(name), full_value(it, name))
                t1, t2, e1, e2, lg, ab, one1, masked, k1, k2, tmp, one2 = (gw[:, s, n] for n in range(12))
                m1, m2, c1, c2, s1, s2, r1, r2 = (gm[:, s, n] for n in range(8))
                iota = repeat(kc[:, K_IOTA:K_IOTA + E], TILES)
                tt, stt = v.tensor_tensor, v.scalar_tensor_tensor

                def first_of(vals, top, c, onehot):
                    tt(onehot, vals, spread(top, E), ALU.is_equal).then_inc(dve_link, 1)
                    dve.wait_ge(dve_link, link_value(it))
                    stt(tmp, onehot, -float(E), iota, ALU.mult, ALU.add).then_inc(dve_link, 1)
                    dve.wait_ge(dve_link, link_value(it))
                    v.tensor_reduce(c, tmp, AX, ALU.min).then_inc(dve_link, 1)
                    dve.wait_ge(dve_link, link_value(it))
                    tt(onehot, tmp, spread(c, E), ALU.is_equal).then_inc(dve_link, 1)
                    dve.wait_ge(dve_link, link_value(it))

                def within(top, t_, keep):
                    tt(tmp, ab, spread(top, E), ALU.max).then_inc(dve_link, 1)
                    dve.wait_ge(dve_link, link_value(it))
                    stt(keep, tmp, 0.02, t_, ALU.mult, ALU.is_ge).then_inc(dve_link, 1)
                    dve.wait_ge(dve_link, link_value(it))

                v.tensor_copy(lg, bank_of(name)[:, 0:TILES * E].rearrange("p (t e) -> p t e", e=E)).then_inc(read_sem(name), 1)
                dve.wait_ge(read_sem(name), read_value(it, name))
                v.reduce_max(m1, lg, AX).then_inc(dve_link, 1)
                dve.wait_ge(dve_link, link_value(it))
                stt(ab, lg, -1.0, lg, ALU.mult, ALU.max).then_inc(dve_link, 1)
                dve.wait_ge(dve_link, link_value(it))
                first_of(lg, m1, c1, one1)
                tt(t1, spread(m1, E), lg, ALU.subtract).then_inc(dve_link, 1)
                dve.wait_ge(dve_link, link_value(it))
                within(m1, t1, k1)
                stt(masked, one1, -1e30, lg, ALU.mult, ALU.add).then_inc(dve_link, 1)
                dve.wait_ge(dve_link, link_value(it))
                v.reduce_max(m2, masked, AX).then_inc(dve_link, 1)
                dve.wait_ge(dve_link, link_value(it))
                first_of(masked, m2, c2, one2)
                tt(t2, spread(m2, E), masked, ALU.subtract).then_inc(dve_link, 1)
                dve.wait_ge(dve_link, link_value(it))
                within(m2, t2, k2)
                dve.sem_inc(gate_in[s].sem, 1)
                yield
                dve.wait_ge(gate_exp[s].sem, gate_exp[s].after(it, 1))
                tt(k1, k1, e1, ALU.mult).then_inc(dve_link, 1)
                dve.wait_ge(dve_link, link_value(it))
                tt(k2, k2, e2, ALU.mult).then_inc(dve_link, 1)
                dve.wait_ge(dve_link, link_value(it))
                v.reduce_sum(s1, k1, AX).then_inc(dve_link, 1)
                dve.wait_ge(dve_link, link_value(it))
                v.reduce_sum(s2, k2, AX).then_inc(dve_link, 1)
                dve.wait_ge(dve_link, link_value(it))
                v.reciprocal(r1, s1).then_inc(dve_link, 1)
                dve.wait_ge(dve_link, link_value(it))
                v.reciprocal(r2, s2).then_inc(dve_link, 1)
                dve.wait_ge(dve_link, link_value(it))
                tt(one1, one1, spread(r1, E), ALU.mult).then_inc(dve_link, 1)
                dve.wait_ge(dve_link, link_value(it))
                tt(one2, one2, spread(r2, E), ALU.mult).then_inc(dve_link, 1)
                dve.wait_ge(dve_link, link_value(it))
                tt(gates[:, s], one1, one2, ALU.add).then_inc(dve_link, 1)
                dve.wait_ge(dve_link, link_value(it))
                yield
                yield

            def ffn(it, f, s):
                inner = (D0, F1)[f]
                total = E * inner
                for n in range(total + FLAG):
                    i = s * total + n
                    if n < total:
                        r = ("h", f, i)
                        f32, old = r32["h"][:, place(r), :], stood_there(r)
                        if f == 1:
                            dve.wait_ge(read_sem(("ga", f, i)), read_value(it, ("ga", f, i)))
                            dve.wait_ge(full_sem(("up", f, i)), full_value(it, ("up", f, i)))
                            v.tensor_tensor(f32, bank_of(("up", f, i))[:], f32, ALU.mult).then_inc(read_sem(("up", f, i)), 1)
                    if n >= FLAG and (n - FLAG) % inner == inner - 1:
                        e = (n - FLAG) // inner
                        name = ("y", f, s * E + e)
                        dve.wait_ge(full_sem(name), full_value(it, name))
                        src = xs if f and e == 0 else ys
                        for ti in range(TILES):
                            last = v.scalar_tensor_tensor(ys[:, s, ti, :], bank_of(name)[:, ti * P:(ti + 1) * P], gates[:, s, ti, e:e + 1],
                                                          src[:, s, ti, :], ALU.mult, ALU.add)
                        last.then_inc(read_sem(name), 1)
                        dve.wait_ge(read_sem(name), read_value(it, name))
                    yield

            def enter(it, s):
                yield from transposed_lo(it, "c", ct, s)
                yield from context_keys(it, s)
                masks(it, s)
                yield from transposed_lo(it, "x0", xt, s)
                yield from single(it, 0, s)
                yield from transposed_lo(it, "x1", xt, s)
                yield from prepare(it, 0, s)

            def between(it, k, s):
                if k == 0:
                    yield from leave(it, 0, s)
                    yield from transposed_lo(it, "x2", xt, s)
                    yield from single(it, 1, s)
                    yield from transposed_lo(it, "x3", xt, s)
                    yield from gates_dense(it, s)
                elif k == 1:
                    norm_stats(it, "l2", s, ys)
                    yield
                    norm_apply(it, "l2", s, ys, xs)
                    yield
                    yield from transposed_lo(it, "x4", xt, s)
                    yield from prepare(it, 1, s)
                elif k == 2:
                    yield from leave(it, 1, s)
                    yield from transposed_lo(it, "x5", xt, s)
                    yield from prepare(it, 2, s)
                elif k == 3:
                    yield from leave(it, 2, s)
                    yield from transposed_lo(it, "x6", xt, s)
                    yield from gates_top2(it, s)
                else:
                    norm_stats(it, "l5", s, ys)
                    yield
                    norm_apply(it, "l5", s, ys, xs)
                    yield

            for sig in all_read:
                dve.sem_inc(sig.sem, 1)
            yf = ys[:].rearrange("p s t d -> p (s t d)")
            prep_count = [0]

            def after(ins):
                prep_count[0] += 1
                ins.then_inc(prep_link, 1)
                dve.wait_ge(prep_link, prep_count[0])

            dve.wait_ge(stage_in[0], 16)
            pair_of = lambda ap: ap.rearrange("p (c two) -> p two c", two=2)
            qk = pieces[0][2][:, 0:2 * D]
            wq, tmp = pair_of(qk), pair_of(yf[:, 0:2 * D])
            v.tensor_tensor(tmp[:, 0], wq[:, 0], wq[:, 1], ALU.subtract)
            after(v.tensor_tensor(tmp[:, 1], wq[:, 1], wq[:, 0], ALU.add))
            v.tensor_copy(qk, yf[:, 0:2 * D]).then_inc(rot_done, 1)
            dve.wait_ge(rot_done, 1)
            for n, (o, c, staged) in enumerate(pieces[:SPLIT_BY_TWO]):
                if n == ATTENTION_PIECES:
                    dve.wait_ge(consts_in, 64)
                    v.tensor_copy(ident16[:], kc[:, K_ID:K_ID + P])
                    v.tensor_copy(identb[:], kc[:, K_ID:K_ID + P])
                    v.tensor_copy(negsel[:].rearrange("p j c -> p (j c)"), consts_f32[:, S_SEL:S_SEL + PAIRS * P])
                    v.tensor_copy(ones_rows[:], consts_f32[:, S_ONES:S_ONES + P])
                    v.memset(half[:], -0.5)
                    v.tensor_copy(rb[:], biases_f32[:, 0:R_B2])
                    after(v.tensor_copy(b2[:], biases_f32[:, R_B2:NR]))
                    v.tensor_tensor(rb[32:64], biases_f32[32:64, 0:R_B2], rb[32:64], ALU.subtract)
                    v.tensor_tensor(b2[64:96], biases_f32[64:96, R_B2:NR], b2[64:96], ALU.subtract)
                    for x in range(2):
                        last = v.scalar_tensor_tensor(cb[:, x:x + 1], cb[:, C_PART + x:C_PART + x + 1], kc[:, K_SIGN:K_SIGN + 1], cb[:, x:x + 1], ALU.mult, ALU.add)
                    last.then_inc(small_prep, 1)
                dve.wait_ge(w_hi, n + 1)
                v.tensor_tensor(w[:, 1, o:o + c], staged, w[:, 0, o:o + c], ALU.subtract).then_inc(w_lo, 1)
            with dve.Fori(0, ITERS) as it:
                links[0] = 0
                run(it, {"enter": enter, "between": between, "mha": mha, "ffn": ffn})
            assert links[0] == LINKS, links[0]

        @block.gpsimd
        def _(pool):
            g = nc.gpsimd

            def norm(it, name, s):
                pool.wait_ge(variance[s].sem, variance[s].after(it, name))
                g.tensor_tensor(rstd[:, s, :], ve[:, s, :], half[:], ALU.pow).then_inc(rstd_done[s].sem, 1)
                yield

            def idle(steps):
                for _ in range(steps):
                    yield

            def part_lo(it, r):
                ri = place(r)
                if r[0] == "t":
                    pool.wait_ge(read_sem(r), read_value(it, r))
                elif r[1] == 0:
                    pool.wait_ge(read_sem(("up", *r[1:])), read_value(it, ("up", *r[1:])))
                else:
                    pool.wait_ge(r_hi.sem, r_hi.after(it, r))
                g.tensor_tensor(rhl[r[0]][:, ri, 1, :], r32[r[0]][:, ri, :], rhl[r[0]][:, ri, 0, :], ALU.subtract).then_inc(r_lo[r[0]].sem, 1)

            def mha(it, m, s):
                for n in range(TILES + 3):
                    yield
                    yield
                    for b in range(2):
                        if 2 <= n < TILES + 2:
                            part_lo(it, ("t", m, s * TILES + n - 2, b))
                        yield
                    yield

            def ffn(it, f, s):
                total = E * (D0, F1)[f]
                for n in range(total + FLAG):
                    i = s * total + n
                    if f == 0 and n < total:
                        part_lo(it, ("h", f, i))
                    if f == 1 and 1 <= n <= total:
                        part_lo(it, ("h", f, i - 1))
                    yield

            def enter(it, s):
                yield from idle(8)
                yield from norm(it, "l0", s)
                yield from idle(3)

            def between(it, k, s):
                if k == 0:
                    yield from idle(1)
                    yield from norm(it, "l1", s)
                    yield from idle(14)
                elif k == 1:
                    yield from norm(it, "l2", s)
                    yield from idle(3)
                elif k == 2:
                    yield from idle(1)
                    yield from norm(it, "l3", s)
                    yield from idle(3)
                elif k == 3:
                    yield from norm(it, "la", s)
                    yield from idle(3)
                    yield from norm(it, "lb", s)
                    yield from idle(1)
                    yield from norm(it, "l4", s)
                    yield from idle(5)
                else:
                    yield from norm(it, "l5", s)
                    yield from idle(1)

            for n in range(ATTENTION_PIECES, MIXTURE0_PIECES):
                o, c, staged = pieces[n]
                pool.dma_start(staged, t["weights"][:, o:o + c]).then_inc(stage_in[n], 16)
            last = g.memset(vm[:].rearrange("p a k s c -> p (a k s c)").bitcast(F32), 0.0)
            last = g.memset(mhl[:].rearrange("p a c -> p (a c)"), 0.0)
            last.then_inc(pool_cleared, 1)
            pool.wait_ge(pool_cleared, 1)
            for p in range(2):
                for h in range(VRING):
                    for sq in range(2):
                        for vp in range(2):
                            c = 64 + 32 * p + vp * (4 * VSTEP - VBACK - 64)
                            row = vm[64 * p:64 * p + 64, h, 0, sq, c:c + 4 * (VSTEP + 1)].rearrange("q (g w) -> q g w", g=4)
                            last = g.memset(row[:, :, 0:4 * HD:4], 1.0)
                last.then_inc(pool_cleared, 1)
                pool.wait_ge(pool_cleared, 2 + p)
            def load_piece(n):
                o, c, staged = pieces[n]
                pool.dma_start(staged, t["weights"][:, o:o + c]).then_inc(stage_in[n], 16)

            def split_piece(n):
                o, c, staged = pieces[n]
                pool.wait_ge(stage_in[n], 16)
                g.tensor_copy(w[:, 0, o:o + c], staged).then_inc(pool_split, 1)
                pool.wait_ge(pool_split, 2 * (n - SPLIT_BY_TWO) + 1)
                g.tensor_tensor(w[:, 1, o:o + c], staged, w[:, 0, o:o + c], ALU.subtract).then_inc(pool_split, 1)

            pool.wait_ge(w_lo, ATTENTION_PIECES)
            load_piece(6)
            load_piece(7)
            for s in range(SLOTS):
                pool.wait_ge(w_lo, ATTENTION_PIECES + 2 * (s + 1))
                last = g.memset(kstack[:, s].rearrange("p v g u t -> p (v g u t)").bitcast(F32), 0.0)
            last.then_inc(pool_prep, 1)
            pool.wait_ge(w_lo, SPLIT_BY_TWO)
            load_piece(8)
            split_piece(7)
            split_piece(8)
            with pool.Fori(0, ITERS) as it:
                run(it, {"enter": enter, "between": between, "mha": mha, "ffn": ffn})


EXP_LN = "natural_log_exp_and_others"


def _arrays(inp):
    import numpy as np

    f = {k: np.asarray(a) for k, a in inp.items()}
    rows = np.empty(D, np.int64)
    vcols = np.empty(D, np.int64)
    for h in range(HEADS):
        for i in range(HD):
            rows[row_of(h, i)] = h * HD + i
            vcols[vcol_of(h, i)] = h * HD + i
    qkv = f["L1_attn_w_qkv"]
    bqkv = f["L1_attn_b_qkv"]
    proj = [f["L0_attn_Wq"].T, f["L0_attn_Wk"].T, f["L0_attn_Wv"].T,
            f["L0_ffn_Wq"], f["L0_ffn_Wk"], f["L0_ffn_Wv"], f["L0_ffn_Wo"],
            f["L0_xattn_Wq"].T[:, rows], f["L0_xattn_Wk"].T[:, rows], f["L0_xattn_Wv"].T[:, vcols], f["L0_xattn_Wo"].T[rows],
            qkv[:, 0:D][:, rows], qkv[:, D:2 * D][:, rows], qkv[:, 2 * D:][:, vcols], f["L1_attn_w_out"][rows],
            f["L1_xattn_Wq"][:, rows], f["L1_xattn_Wk"][:, rows], f["L1_xattn_Wv"][rows][:, vcols], f["L1_xattn_Wo"]]
    weights = np.concatenate(proj + [
        f["L0_ffn_Wg"], f["L1_ffn_router_w"].T,
        f["L0_ffn_W1"].transpose(1, 0, 2).reshape(D, -1),
        f["L0_ffn_W2"].reshape(E, D0, P, D).transpose(2, 0, 1, 3).reshape(P, -1),
        f["L1_ffn_w_gate"].transpose(2, 0, 1).reshape(D, -1),
        f["L1_ffn_w_up"].transpose(2, 0, 1).reshape(D, -1),
        f["L1_ffn_w_down"].transpose(2, 0, 1).reshape(F1, P, E, D).transpose(1, 2, 0, 3).reshape(P, -1)], axis=1)
    assert weights.shape == (P, NW)
    row_bias = np.zeros((P, NR), np.float32)
    vecs = [f["L0_attn_bv"], f["L0_ffn_bv"], f["L0_ffn_bo"],
            f["L0_xattn_bv"][vcols], f["L0_xattn_bo"], bqkv[2 * D:][vcols], f["L1_attn_b_out"],
            f["L1_xattn_bv"][vcols], f["L1_xattn_bo"], f["L0_ffn_bg"]]
    for r in (0, 32):
        row_bias[r, 0:R_B2] = np.concatenate(vecs)
    for r in (0, 32, 64):
        row_bias[r:r + E, R_B2:] = f["L0_ffn_b2"]
    partner = np.arange(D) ^ 1
    col = [f["L0_attn_bq"], f["L0_attn_bk"], f["L0_ffn_bq"], f["L0_ffn_bk"],
           f["L0_xattn_bq"][rows], f["L0_xattn_bk"][rows], bqkv[0:D][rows], bqkv[D:2 * D][rows],
           f["L1_xattn_bq"][rows], f["L1_xattn_bk"][rows]]
    col_bias = np.concatenate([np.stack(col, 1), f["L0_ffn_b1"].reshape(E * D0, P).T,
                               np.stack([f["L0_attn_bq"][partner], f["L0_attn_bk"][partner]], 1)], axis=1)
    k, k16 = np.zeros((P, NK), np.float32), np.zeros((P, NS), np.float32)
    k[:, K_ID:K_ID + P] = np.eye(P)
    k[np.arange(P), K_PERM + rows] = 1
    seq = np.arange(P) // SEQ
    k[:, K_CROSS:K_CROSS + P] = np.where(seq[:, None] == seq[None, :], 0.0, -1e30)
    half_dim = D // 2
    inv = np.float32(10000.0) ** (np.arange(0, half_dim, 2, dtype=np.float32) / np.float32(half_dim))
    rad = np.arange(SEQ, dtype=np.float32)[:, None] / inv
    table = np.repeat(np.stack((np.sin(rad), np.cos(rad)), axis=-1).reshape(SEQ, -1), 2, axis=-1)
    k[:, K_ROPE:K_ROPE + SEQ] = table.T
    for j in range(PAIRS):
        for p in range(2):
            r = 4 * (j % 4) + 2 * (j // 4) + p
            c = S_SEL + j * P + 64 * p
            k16[[r, HEADS + r], c:c + 64] = -1
    k16[[0, 32], S_ONES:S_ONES + P] = 1
    k[:, K_SIGN] = np.where(np.arange(P) % 2 == 0, -1, 1)
    k[:, K_IOTA:K_IOTA + E] = np.arange(E)
    for n, name in enumerate(("g0", "b0", "g1", "b1")):
        k[:, K_LN + n * D:K_LN + (n + 1) * D] = f["L1_xattn_" + name][None, :]
    mask = f["mask_BxS2_bf1"].view(np.uint8)
    return {
        "x": f["x"].reshape(TOKENS, D), "ctx": f["ctx_1024"].reshape(TOKENS, D),
        "mask_row": mask.reshape(1, TOKENS), "mask_cols": np.concatenate([mask.T, mask.T], axis=0),
        "weights": weights, "row_bias": row_bias, "col_bias": col_bias, "consts": k, "consts16": k16,
    }


def kernel(**inputs):
    import numpy as _np
    import concourse.bacc as _bacc
    from concourse.bass_utils import run_bass_kernel_spmd as _run

    nc = _bacc.Bacc("TRN2", target_bir_lowering=False, num_devices=1)
    arrays, t = {}, {}
    for name, a in _arrays(inputs).items():
        a = _np.ascontiguousarray(a)
        arrays["in_" + name] = a
        t[name] = nc.dram_tensor("in_" + name, a.shape, mybir.dt.from_np(a.dtype), kind="ExternalInput").ap()
    t["out"] = nc.dram_tensor("out", (TOKENS, D), F32, kind="ExternalOutput").ap()
    build(nc, t)
    r = _run(nc, [arrays], core_ids=[0])
    return r.results[0]["out"].reshape(BATCH, SEQ, D)
```
